# Optimizing a Trainium2 kernel written in Bass

```python
import numpy as np
import jax
import jax.numpy as jnp

def _softmax(x, axis=-1):
    return jax.nn.softmax(x, axis=axis)
def _gelu(x):
    return jax.nn.gelu(x, approximate=True)
def _silu(x):
    return jax.nn.silu(x)
def _sigmoid(x):
    return jax.nn.sigmoid(x)
def _layernorm(x, axis=-1, eps=1e-5):
    m = jnp.mean(x, axis=axis, keepdims=True)
    v = jnp.var(x, axis=axis, keepdims=True)
    return (x - m) / jnp.sqrt(v + eps)
def _scatter_add(tgt, idx, src, axis=0):
    return tgt.at[idx].add(src)
def _segment_sum(src, seg, n):
    return jax.ops.segment_sum(src, seg, n)

kernel_name = 'mk_adj_resnorm_d4_adj_256_f72656'

def setup_inputs(seed: int = 0):
    np.random.seed(seed)
    _w = jnp.asarray
    def _rec_inputs():
        import jax
        import jax.numpy as jnp
        _gk = jax.random.key(seed)
        x = -8.015e-05 + 0.9999 * jax.random.normal(jax.random.fold_in(_gk, 1), (16, 1024, 256), jnp.float32)
        _w = (1.0 + jnp.arange(1024, dtype=jnp.float32)) ** -0.5
        _w = _w / _w.mean()
        _pij = jnp.clip(0.015625 * _w[:, None] * _w[None, :], 0.0, 1.0)
        _a = jax.random.uniform(jax.random.fold_in(_gk, 2), (16, 1024, 1024)) < _pij
        _a = jnp.logical_or(_a, jnp.swapaxes(_a, -1, -2))
        _a = jnp.logical_or(_a, jnp.eye(1024, dtype=bool))
        _af = _a.astype(jnp.float32)
        _af = _af * jax.random.uniform(jax.random.fold_in(_gk, 3), (16, 1024, 1024), jnp.float32, 0.05, 0.999837)
        adj = _af
        return x, adj
    x, adj = _rec_inputs()
    def _L0_gnn_setup():
        import jax, jax.numpy as jnp
        import numpy as np
        GROUPS = [list(range(25)), [0, 1, 2, 3, 4, 5, 6, 7, 8], [0, 9, 10, 11, 12, 13, 14], [6, 7, 8, 12, 13, 14], [3, 4, 5, 9, 10, 11]]
        B, N, D_IN, D_HID = (8192, 25, 256, 512)

        def _graph_conv(x, adj, W, b):
            n = adj.shape[-1]
            A = adj + jnp.eye(n, dtype=adj.dtype)
            deg = jnp.sum(A, axis=-1)
            deg_safe = jnp.where(deg == 0, 1.0, deg)
            dinv = jnp.where(deg == 0, 0.0, deg_safe ** (-0.5))
            norm_adj = dinv[:, :, None] * A * dinv[:, None, :]
            support = jnp.einsum('bnd,de->bne', x, W)
            out = jnp.einsum('bnm,bme->bne', norm_adj, support) + b
            return jax.nn.relu(out)
        key = jax.random.key(seed)
        ks = jax.random.split(key, 7)
        s1 = float(np.sqrt(6.0 / (D_IN + D_HID)))
        s2 = float(np.sqrt(6.0 / (D_HID + D_IN)))
        return {'x': jax.random.normal(ks[0], (B, N, D_IN), dtype=jnp.float32), 'adj': jax.random.uniform(ks[1], (B, N, N), dtype=jnp.float32), 'W1': jax.random.uniform(ks[2], (5, D_IN, D_HID), jnp.float32, -s1, s1), 'b1': jnp.zeros((5, D_HID), dtype=jnp.float32), 'W2': jax.random.uniform(ks[3], (5, D_HID, D_IN), jnp.float32, -s2, s2), 'b2': jnp.zeros((5, D_IN), dtype=jnp.float32), 'fusion_w': jnp.ones((5,), dtype=jnp.float32)}
    _L0_gnn_all = _L0_gnn_setup()
    _L0_gnn_in = {k: v for k, v in _L0_gnn_all.items() if k in ('W1', 'b1', 'W2', 'b2', 'fusion_w', )}
    del _L0_gnn_all

    def _L1_gnn_setup():
        import jax, jax.numpy as jnp
        import numpy as np
        B, N, IN_F, OUT_F = (2, 4096, 256, 256)
        ALPHA = 0.2
        MASK_NEG = -9000000000000000.0
        SINK_NEG = -1000000000.0
        key = jax.random.key(seed)
        kx, kadj, kw, kbw, kai, kbi, kaj, kbj = jax.random.split(key, 8)
        x = jax.random.normal(kx, (B, N, IN_F), dtype=jnp.float32)
        adjs = (jax.random.uniform(kadj, (B, N, N)) < 0.01).astype(jnp.float32)

        def xavier(k, shape, gain=1.414):
            fan_out, fan_in = shape
            bound = gain * np.sqrt(6.0 / (fan_in + fan_out))
            return jax.random.uniform(k, shape, minval=-bound, maxval=bound, dtype=jnp.float32)
        W = xavier(kw, (OUT_F, IN_F))
        bW = jax.random.uniform(kbw, (OUT_F,), minval=-1 / np.sqrt(IN_F), maxval=1 / np.sqrt(IN_F), dtype=jnp.float32)
        wai = xavier(kai, (1, OUT_F))
        bai = jax.random.uniform(kbi, (1,), minval=-1 / np.sqrt(OUT_F), maxval=1 / np.sqrt(OUT_F), dtype=jnp.float32)
        waj = xavier(kaj, (1, OUT_F))
        baj = jax.random.uniform(kbj, (1,), minval=-1 / np.sqrt(OUT_F), maxval=1 / np.sqrt(OUT_F), dtype=jnp.float32)
        return {'x': x, 'adjs': adjs, 'W': W, 'bW': bW, 'wai': wai, 'bai': bai, 'waj': waj, 'baj': baj}
    _L1_gnn_all = _L1_gnn_setup()
    _L1_gnn_in = {k: v for k, v in _L1_gnn_all.items() if k in ('W', 'bW', 'wai', 'bai', 'waj', 'baj', )}
    del _L1_gnn_all

    def _L2_gnn_setup():
        import jax, jax.numpy as jnp
        import numpy as np
        D_IN = 256
        D_HID = 512
        key = jax.random.key(seed)
        k1, k2, k3, k4, k5, k6 = jax.random.split(key, 6)
        x = jax.random.normal(k1, (8, 4096, D_IN), dtype=jnp.float32)
        adj = jax.random.uniform(k2, (8, 4096, 4096), dtype=jnp.float32)
        s1 = 1.0 / np.sqrt(D_IN)
        s2 = 1.0 / np.sqrt(D_HID)
        W1 = jax.random.uniform(k3, (D_IN, D_HID), dtype=jnp.float32, minval=-s1, maxval=s1)
        b1 = jax.random.uniform(k4, (D_HID,), dtype=jnp.float32, minval=-s1, maxval=s1)
        W2 = jax.random.uniform(k5, (D_HID, D_IN), dtype=jnp.float32, minval=-s2, maxval=s2)
        b2 = jax.random.uniform(k6, (D_IN,), dtype=jnp.float32, minval=-s2, maxval=s2)
        eps = jnp.zeros((1,), dtype=jnp.float32)
        return {'x': x, 'adj': adj, 'eps': eps, 'W1': W1, 'b1': b1, 'W2': W2, 'b2': b2}
    _L2_gnn_all = _L2_gnn_setup()
    _L2_gnn_in = {k: v for k, v in _L2_gnn_all.items() if k in ('eps', 'W1', 'b1', 'W2', 'b2', )}
    del _L2_gnn_all

    def _L3_gnn_setup():
        import jax, jax.numpy as jnp
        import numpy as np
        B, N, D, H = (8, 2048, 256, 1024)
        RMS_EPS = 1e-06

        def _rmsnorm(h, w, eps=RMS_EPS):
            var = jnp.mean(jnp.square(h), axis=-1, keepdims=True)
            return h * jax.lax.rsqrt(var + eps) * w
        key = jax.random.key(seed)
        ks = jax.random.split(key, 5)
        x = jax.random.normal(ks[0], (B, N, D), dtype=jnp.float32)
        adjacency = jax.random.uniform(ks[1], (B, N, N), dtype=jnp.float32)
        epsilon = jnp.zeros((), dtype=jnp.float32)
        W1 = jax.random.normal(ks[2], (D, H), dtype=jnp.float32) * (1.0 / np.sqrt(D))
        b1 = jnp.zeros((H,), dtype=jnp.float32)
        rms_weight = jnp.ones((H,), dtype=jnp.float32)
        W2 = jax.random.normal(ks[3], (H, D), dtype=jnp.float32) * (1.0 / np.sqrt(H))
        b2 = jnp.zeros((D,), dtype=jnp.float32)
        return {'x': x, 'adjacency': adjacency, 'epsilon': epsilon, 'W1': W1, 'b1': b1, 'rms_weight': rms_weight, 'W2': W2, 'b2': b2}
    _L3_gnn_all = _L3_gnn_setup()
    _L3_gnn_in = {k: v for k, v in _L3_gnn_all.items() if k in ('epsilon', 'W1', 'b1', 'rms_weight', 'W2', 'b2', )}
    del _L3_gnn_all

    return {
        "x": x,
        "adj": adj,
        "L0_gnn_W1": _L0_gnn_in["W1"],
        "L0_gnn_b1": _L0_gnn_in["b1"],
        "L0_gnn_W2": _L0_gnn_in["W2"],
        "L0_gnn_b2": _L0_gnn_in["b2"],
        "L0_gnn_fusion_w": _L0_gnn_in["fusion_w"],
        "L1_gnn_W": _L1_gnn_in["W"],
        "L1_gnn_bW": _L1_gnn_in["bW"],
        "L1_gnn_wai": _L1_gnn_in["wai"],
        "L1_gnn_bai": _L1_gnn_in["bai"],
        "L1_gnn_waj": _L1_gnn_in["waj"],
        "L1_gnn_baj": _L1_gnn_in["baj"],
        "L2_gnn_eps": _L2_gnn_in["eps"],
        "L2_gnn_W1": _L2_gnn_in["W1"],
        "L2_gnn_b1": _L2_gnn_in["b1"],
        "L2_gnn_W2": _L2_gnn_in["W2"],
        "L2_gnn_b2": _L2_gnn_in["b2"],
        "L3_gnn_epsilon": _L3_gnn_in["epsilon"],
        "L3_gnn_W1": _L3_gnn_in["W1"],
        "L3_gnn_b1": _L3_gnn_in["b1"],
        "L3_gnn_rms_weight": _L3_gnn_in["rms_weight"],
        "L3_gnn_W2": _L3_gnn_in["W2"],
        "L3_gnn_b2": _L3_gnn_in["b2"],
    }

def reference(x, adj, L0_gnn_W1, L0_gnn_b1, L0_gnn_W2, L0_gnn_b2, L0_gnn_fusion_w, L1_gnn_W, L1_gnn_bW, L1_gnn_wai, L1_gnn_bai, L1_gnn_waj, L1_gnn_baj, L2_gnn_eps, L2_gnn_W1, L2_gnn_b1, L2_gnn_W2, L2_gnn_b2, L3_gnn_epsilon, L3_gnn_W1, L3_gnn_b1, L3_gnn_rms_weight, L3_gnn_W2, L3_gnn_b2):
    import jax
    import jax.numpy as jnp
    def _L0_gnn_ref(x, adj, W1, b1, W2, b2, fusion_w):
        import jax, jax.numpy as jnp
        import numpy as np
        GROUPS = [list(range(25)), [0, 1, 2, 3, 4, 5, 6, 7, 8], [0, 9, 10, 11, 12, 13, 14], [6, 7, 8, 12, 13, 14], [3, 4, 5, 9, 10, 11]]
        B, N, D_IN, D_HID = (8192, 25, 256, 512)

        def _graph_conv(x, adj, W, b):
            n = adj.shape[-1]
            A = adj + jnp.eye(n, dtype=adj.dtype)
            deg = jnp.sum(A, axis=-1)
            deg_safe = jnp.where(deg == 0, 1.0, deg)
            dinv = jnp.where(deg == 0, 0.0, deg_safe ** (-0.5))
            norm_adj = dinv[:, :, None] * A * dinv[:, None, :]
            support = jnp.einsum('bnd,de->bne', x, W)
            out = jnp.einsum('bnm,bme->bne', norm_adj, support) + b
            return jax.nn.relu(out)
        norm_w = jax.nn.softmax(fusion_w)
        fused = jnp.zeros_like(x)
        for g, idx_list in enumerate(GROUPS):
            idx = jnp.asarray(idx_list)
            x_g = x[:, idx, :]
            adj_g = adj[:, idx][:, :, idx]
            h = _graph_conv(x_g, adj_g, W1[g], b1[g])
            out_g = _graph_conv(h, adj_g, W2[g], b2[g])
            fused = fused.at[:, idx, :].add(norm_w[g] * out_g)
        return fused

    def _L1_gnn_ref(x, adjs, W, bW, wai, bai, waj, baj):
        import jax, jax.numpy as jnp
        import numpy as np
        B, N, IN_F, OUT_F = (2, 4096, 256, 256)
        ALPHA = 0.2
        MASK_NEG = -9000000000000000.0
        SINK_NEG = -1000000000.0
        b, n, _ = adjs.shape
        z = jnp.einsum('bni,oi->bno', x, W) + bW
        ai = jnp.einsum('bno,ko->bnk', z, wai) + bai
        aj = jnp.einsum('bno,ko->bnk', z, waj) + baj
        e = ai + jnp.swapaxes(aj, 1, 2)
        e = jnp.where(e >= 0, e, ALPHA * e)
        att = jnp.where(adjs > 0, e, MASK_NEG)
        sink = jnp.full((b, n, 1), SINK_NEG, dtype=att.dtype)
        att = jax.nn.softmax(jnp.concatenate([att, sink], axis=-1), axis=-1)[:, :, :n]
        return jnp.einsum('bnm,bmo->bno', att, z)

    def _L2_gnn_ref(x, adj, eps, W1, b1, W2, b2):
        import jax, jax.numpy as jnp
        import numpy as np
        D_IN = 256
        D_HID = 512
        aggregated = jnp.einsum('bnm,bmd->bnd', adj, x)
        h = (1.0 + eps) * x + aggregated
        h = jax.nn.relu(h @ W1 + b1)
        return h @ W2 + b2

    def _L3_gnn_ref(x, adjacency, epsilon, W1, b1, rms_weight, W2, b2):
        import jax, jax.numpy as jnp
        import numpy as np
        B, N, D, H = (8, 2048, 256, 1024)
        RMS_EPS = 1e-06

        def _rmsnorm(h, w, eps=RMS_EPS):
            var = jnp.mean(jnp.square(h), axis=-1, keepdims=True)
            return h * jax.lax.rsqrt(var + eps) * w
        neighbor_sum = jnp.einsum('bnm,bmd->bnd', adjacency, x)
        agg = epsilon * x + neighbor_sum
        h = jnp.einsum('bnd,dh->bnh', agg, W1) + b1
        h = jax.nn.silu(_rmsnorm(h, rms_weight))
        out = jnp.einsum('bnh,hd->bnd', h, W2) + b2
        return out

    x = _layernorm(x + _L0_gnn_ref(x, adj, L0_gnn_W1, L0_gnn_b1, L0_gnn_W2, L0_gnn_b2, L0_gnn_fusion_w), axis=-1)
    x = _layernorm(x + _L1_gnn_ref(x, adj, L1_gnn_W, L1_gnn_bW, L1_gnn_wai, L1_gnn_bai, L1_gnn_waj, L1_gnn_baj), axis=-1)
    x = _layernorm(x + _L2_gnn_ref(x, adj, L2_gnn_eps, L2_gnn_W1, L2_gnn_b1, L2_gnn_W2, L2_gnn_b2), axis=-1)
    x = _layernorm(x + _L3_gnn_ref(x, adj, L3_gnn_epsilon, L3_gnn_W1, L3_gnn_b1, L3_gnn_rms_weight, L3_gnn_W2, L3_gnn_b2), axis=-1)
    return x


_drawn_inputs = setup_inputs


def setup_inputs(seed=0):
    import zlib

    import numpy as np

    out = dict(_drawn_inputs(seed))
    spreads = {'L0_gnn_b1': (0.0, 0.744),
     'L0_gnn_b2': (0.0, 0.8),
     'L0_gnn_fusion_w': (1.0, 0.6),
     'L3_gnn_b1': (0.0, 0.8),
     'L3_gnn_rms_weight': (1.0, 0.2),
     'L3_gnn_b2': (0.0, 0.1)}
    factors = {'L0_gnn_W1': 3.094, 'L2_gnn_b1': 6.319, 'L2_gnn_b2': 2.902}
    for name, (base, spread) in spreads.items():
        noise = np.random.default_rng([zlib.crc32(name.encode()), seed]).standard_normal(out[name].shape)
        drawn = base * np.exp(spread * noise) if base else spread * noise
        out[name] = jnp.asarray(drawn.astype(out[name].dtype))
    for name, factor in factors.items():
        out[name] = (out[name] * factor).astype(out[name].dtype)
    return out
```

```python
from contextlib import ExitStack

import concourse.bass as bass
from concourse import mybir

F32 = mybir.dt.float32
F32R = mybir.dt.float32r
BF16 = mybir.dt.bfloat16
ALU = mybir.AluOpType
ACT = mybir.ActivationFunctionType
AX = mybir.AxisListType

P = 128
GRAPHS, NODES, D = 16, 1024, 256
NT = NODES // P
DT = D // P
HALF = 512
QUARTER = 256
NQ = NODES // QUARTER
HID2, HID3 = 512, 1024
HT2, HT3 = HID2 // P, HID3 // P
LN_EPS, RMS_EPS = 1e-5, 1e-6
SLOPE = 0.2
MASKED, SINK = -9.0e15, -1.0e9

L0_NODES, L0_HID = 25, 512
GROUP_RUNS = [[(0, 25)], [(0, 9)], [(0, 1), (9, 6)], [(6, 3), (12, 3)], [(3, 3), (9, 3)]]
NG = len(GROUP_RUNS)
PAD = 32
PER = P // PAD
T0 = GRAPHS // PER


def group_size(g):
    return sum(n for _, n in GROUP_RUNS[g])


def row(ap):
    return ap.rearrange("(a n) -> a n", a=1)


def adj_resnorm(nc, x, adj, L0_W1, L0_b1, L0_W2, L0_b2, L0_fusion_w, W, bW, wai, bai, waj, baj,
                eps2, L2_W1, L2_b1, L2_W2, L2_b2, eps3, L3_W1, L3_b1, rms_w, L3_W2, L3_b2, out):
    x_l0 = nc.dram_tensor("x_after_l0", (GRAPHS, L0_NODES, D), F32, kind="Internal").ap()

    with ExitStack() as ctx:
        def sb(name, shape, dt=F32, c=ctx):
            return c.enter_context(nc.sbuf_tensor(name, shape, dt))

        def sem(name):
            return ctx.enter_context(nc.semaphore(name))

        ident = sb("ident", [P, P])
        ones = sb("ones", [P, P])
        WT_hi, WT_lo = sb("WT_hi", [P, DT, D], F32R), sb("WT_lo", [P, DT, D], F32R)
        W12_hi, W12_lo = sb("W12_hi", [P, DT, HID2], F32R), sb("W12_lo", [P, DT, HID2], F32R)
        W13_hi, W13_lo = sb("W13_hi", [P, DT, HID3], F32R), sb("W13_lo", [P, DT, HID3], F32R)
        W22 = sb("W22", [P, HT2, D])
        W23 = sb("W23", [P, HT3, D])
        b12 = sb("b12", [P, HT2])
        b13 = sb("b13", [P, HT3])
        rms_col = sb("rms_col", [P, HT3])
        bW_row = sb("bW_row", [P, D])
        b22_row = sb("b22_row", [P, D])
        b23_row = sb("b23_row", [P, D])
        v_rows = sb("v_rows", [P, 2, D])
        c_cols = sb("c_cols", [P, 2])
        cI2_hi, cI2_lo = sb("cI2_hi", [P, P], F32R), sb("cI2_lo", [P, P], F32R)
        cI3 = sb("cI3", [P, P])
        neg_half = sb("neg_half", [P, 20])

        banks = [ctx.enter_context(nc.psum_tensor(f"bank{i}", [P, HALF], F32)) for i in range(8)]

        prologue(nc, ctx, sem, banks, ident, ones, WT_hi, WT_lo, W12_hi, W12_lo, W13_hi, W13_lo,
                 W22, W23, b12, b13, rms_col, bW_row, b22_row, b23_row, v_rows, c_cols,
                 cI2_hi, cI2_lo, cI3, neg_half,
                 x, adj, L0_W1, L0_b1, L0_W2, L0_b2, L0_fusion_w, W, bW, wai, bai, waj, baj,
                 eps2, L2_W1, L2_b1, L2_W2, L2_b2, eps3, L3_W1, L3_b1, rms_w, L3_W2, L3_b2, x_l0)
        layers(nc, sb, sem, banks, ident, ones, WT_hi, WT_lo, W12_hi, W12_lo, W13_hi, W13_lo,
               W22, W23, b12, b13, rms_col, bW_row, b22_row, b23_row, v_rows, c_cols,
               cI2_hi, cI2_lo, cI3, neg_half, x, adj, x_l0, out)


def prologue(nc, ctx, sem, banks, ident, ones, WT_hi, WT_lo, W12_hi, W12_lo, W13_hi, W13_lo,
             W22, W23, b12, b13, rms_col, bW_row, b22_row, b23_row, v_rows, c_cols,
             cI2_hi, cI2_lo, cI3, neg_half,
             x, adj, L0_W1, L0_b1, L0_W2, L0_b2, L0_fusion_w, W, bW, wai, bai, waj, baj,
             eps2, L2_W1, L2_b1, L2_W2, L2_b2, eps3, L3_W1, L3_b1, rms_w, L3_W2, L3_b2, x_l0):
    ROWS = T0 * P
    KH = L0_HID // P
    with ExitStack() as pro:
        def sb(name, shape, dt=F32):
            return pro.enter_context(nc.sbuf_tensor(name, shape, dt))

        W_nat = sb("W_nat", [P, DT, D])
        W12_f, W13_f = sb("W12_f", [P, DT, HID2]), sb("W13_f", [P, DT, HID3])
        wa_cols = sb("wa_cols", [P, 2, DT])
        bW_col = sb("bW_col", [P, DT])
        ba = sb("ba", [P, 2])
        eps_col = sb("eps_col", [P, 2])
        one_eps2 = sb("one_eps2", [P, 1])
        cI2 = sb("cI2", [P, P])
        fus, fus_e = sb("fus", [P, NG]), sb("fus_e", [P, NG])
        fus_m, fus_s, fus_r = sb("fus_m", [P, 1]), sb("fus_s", [P, 1]), sb("fus_r", [P, 1])
        row_mask = sb("row_mask", [1, NG, PER, PAD])
        mw = sb("mw", [P, NG])
        G1 = sb("G1", [P, NG, DT, L0_HID])
        G2 = sb("G2", [P, NG, KH, D])
        g_b1 = sb("g_b1", [P, NG, KH])
        g_b2 = sb("g_b2", [P, NG, D])
        X0 = sb("X0", [P, T0, D])
        A0 = sb("A0", [P, NG, T0 * PER, PAD])
        deg, deg0 = sb("deg", [P, NG * T0]), sb("deg0", [P, NG * T0])
        dinv, dtmp = sb("dinv", [P, NG * T0]), sb("dtmp", [P, NG * T0])
        AT = sb("AT", [P, NG, T0, P])
        XaT = [sb(f"XaT{g}", [P, DT, GRAPHS * group_size(g)]) for g in range(NG)]
        H1 = sb("H1", [P, 2, KH, T0 * PER, PAD])
        Z = sb("Z", [P, 2, T0, D])
        Ot = sb("Ot", [P, 2, D])
        Or = sb("Or", [P, 2, D])

        s_wload = sem("p_weights_loaded")
        s_cload = sem("p_columns_loaded")
        s_gload = sem("p_group_weights_loaded")
        s_zero = sem("p_zeroed")
        s_ident = sem("p_identity")
        s_aload = sem("p_graphs_loaded")
        s_mm = sem("p_bank_written")
        s_ev = sem("p_bank_read")
        s_hmm = sem("p_hidden_written")
        s_hev = sem("p_hidden_read")
        s_dve = sem("p_vector_steps")
        s_mask = sem("p_masks")
        s_deg = sem("p_degrees")
        s_pow = sem("p_powers")
        s_fus = sem("p_fusion_exp")
        s_or = sem("p_group_relu")
        s_acc = sem("p_accumulated")
        s_store = sem("p_stored")

        w_loads, c_loads, a_loads = 5, 15, 2 * GRAPHS
        supports = 4 + NG + DT * NG

        with nc.Block() as block:
            @block.sync
            def _(sp):
                sp.wait_ge(s_zero, 2)
                for b in range(GRAPHS):
                    t, i = b // PER, b % PER
                    rows = slice(PAD * i, PAD * i + L0_NODES)
                    sp.dma_start(A0[rows, 0, b, 0:L0_NODES],
                                 adj[b, 0:L0_NODES, 0:L0_NODES]).then_inc(s_aload, 16)
                    sp.dma_start(X0[rows, t, :], x[b, 0:L0_NODES, :]).then_inc(s_aload, 16)
                sp.dma_start(G1[:], L0_W1.rearrange("g (t p) n -> p g t n", p=P)).then_inc(s_gload, 16)
                sp.dma_start(G2[:], L0_W2.rearrange("g (t p) n -> p g t n", p=P)).then_inc(s_gload, 16)
                sp.dma_start(W12_f[:], L2_W1.rearrange("(t p) n -> p t n", p=P)).then_inc(s_wload, 16)
                sp.dma_start(W13_f[:], L3_W1.rearrange("(t p) n -> p t n", p=P)).then_inc(s_wload, 16)
                sp.dma_start(W22[:], L2_W2.rearrange("(t p) n -> p t n", p=P)).then_inc(s_wload, 16)
                sp.dma_start(W23[:], L3_W2.rearrange("(t p) n -> p t n", p=P)).then_inc(s_wload, 16)
                sp.wait_ge(s_acc, NG * T0)
                for b in range(GRAPHS):
                    t, i = b // PER, b % PER
                    rows = slice(PAD * i, PAD * i + L0_NODES)
                    sp.dma_start(x_l0[b], X0[rows, t, :]).then_inc(s_store, 16)
                sp.wait_ge(s_store, 16 * GRAPHS)
                sp.wait_ge(s_wload, 16 * w_loads)

            @block.scalar
            def _(act):
                act.dma_start(W_nat[:], W.rearrange("(t p) n -> p t n", p=P)).then_inc(s_wload, 16)

                def column(dst, src):
                    act.dma_start(dst, src).then_inc(s_cload, 16)

                with nc.allow_non_contiguous_dma(reason="small columns"):
                    column(wa_cols[:, 0, :], wai.rearrange("a (t p) -> p (a t)", p=P))
                    column(wa_cols[:, 1, :], waj.rearrange("a (t p) -> p (a t)", p=P))
                    column(bW_col[:], bW.rearrange("(t p) -> p t", p=P))
                    column(b12[:], L2_b1.rearrange("(t p) -> p t", p=P))
                    column(b13[:], L3_b1.rearrange("(t p) -> p t", p=P))
                    column(rms_col[:], rms_w.rearrange("(t p) -> p t", p=P))
                    column(g_b1[:], L0_b1.rearrange("g (t p) -> p g t", p=P))
                    column(ba[:, 0:1], row(bai).to_broadcast([P, 1]))
                    column(ba[:, 1:2], row(baj).to_broadcast([P, 1]))
                    column(eps_col[:, 0:1], row(eps2).to_broadcast([P, 1]))
                    column(eps_col[:, 1:2], row(eps3).to_broadcast([P, 1]))
                    column(fus[:], row(L0_fusion_w).to_broadcast([P, NG]))
                    column(bW_row[:], row(bW).to_broadcast([P, D]))
                    column(b22_row[:], row(L2_b2).to_broadcast([P, D]))
                    column(b23_row[:], row(L3_b2).to_broadcast([P, D]))
                    act.dma_start(g_b2[:], L0_b2.rearrange("(a g) n -> a g n", a=1).to_broadcast([P, NG, D]))\
                       .then_inc(s_gload, 16)
                act.wait_ge(s_dve, 2)
                nc.scalar.activation(fus_e[:], fus[:], ACT.Exp, bias=fus_m[:], accum_out=fus_s[:]).then_inc(s_fus, 1)
                def hidden_rows(g):
                    for h in range(KH):
                        n = g * KH + h
                        if g >= 2 and h == 0:
                            act.wait_ge(s_mm, supports + 2 * T0 * (g - 2) + T0)
                        act.wait_ge(s_hmm, n + 1)
                        if n == 0:
                            act.wait_ge(s_zero, 3)
                        at = 0
                        for first, size in GROUP_RUNS[g]:
                            src = banks[6 + n % 2][:, 0:GRAPHS * group_size(g)]\
                                .rearrange("p (b j) -> p b j", b=GRAPHS)[:, :, at:at + size]
                            last = nc.scalar.activation(H1[:, g % 2, h, :, first:first + size], src,
                                                        ACT.Relu, bias=g_b1[:, g, h:h + 1])
                            at += size
                        last.then_inc(s_hev, 1)

                hidden_rows(0)
                hidden_rows(1)
                for g in range(NG):
                    for t in range(T0):
                        i = g * T0 + t
                        act.wait_ge(s_ev, supports + 2 * T0 * g + T0 + t + 1)
                        if i >= 2:
                            act.wait_ge(s_acc, i - 1)
                        nc.scalar.activation(Or[:, i % 2, :], Ot[:, i % 2, :], ACT.Relu,
                                             scale=mw[:, g:g + 1]).then_inc(s_or, 1)
                    if g + 2 < NG:
                        hidden_rows(g + 2)

            @block.gpsimd
            def _(pool):
                nc.gpsimd.memset(A0[:, 0], 0.0).then_inc(s_zero, 1)
                nc.gpsimd.memset(X0[:], 0.0).then_inc(s_zero, 1)
                nc.gpsimd.memset(ident[:], 0.0).then_inc(s_ident, 1)
                nc.gpsimd.memset(ones[:], 1.0).then_inc(s_ident, 1)
                nc.gpsimd.memset(neg_half[:], -0.5).then_inc(s_ident, 1)
                pool.wait_ge(s_ident, 3)
                nc.gpsimd.affine_select(out=ident[:], in_=ident[:], compare_op=ALU.not_equal, fill=1.0, base=0,
                                        pattern=[[-1, P]], channel_multiplier=1).then_inc(s_ident, 1)
                nc.gpsimd.memset(H1[:], 0.0).then_inc(s_zero, 1)
                pool.wait_ge(s_deg, 1)
                nc.gpsimd.tensor_tensor(dtmp[:], dinv[:], neg_half[:], ALU.pow).then_inc(s_pow, 1)
                for i in range(NG * T0):
                    pool.wait_ge(s_or, i + 1)
                    if i >= T0:
                        pool.wait_ge(s_acc, i - T0 + 1)
                    nc.gpsimd.tensor_tensor(X0[:, i % T0, :], X0[:, i % T0, :], Or[:, i % 2, :],
                                            ALU.add).then_inc(s_acc, 1)

            @block.vector
            def _(dve):
                steps = [0]

                def step(ins):
                    steps[0] += 1
                    ins.then_inc(s_dve, 1)
                    dve.wait_ge(s_dve, steps[0])

                dve.wait_ge(s_cload, 16 * c_loads)
                step(nc.vector.reduce_max(fus_m[:], fus[:], axis=AX.X))
                step(nc.vector.tensor_scalar(fus_m[:], fus_m[:], -1.0, None, ALU.mult))
                step(nc.vector.memset(row_mask[:], 0.0))
                for g in range(NG):
                    for first, size in GROUP_RUNS[g]:
                        last = nc.vector.memset(row_mask[:, g, :, first:first + size], 1.0)
                last.then_inc(s_mask, 1)
                step(nc.vector.memset(A0[:, 1:NG], 0.0))
                dve.wait_ge(s_aload, 16 * a_loads)
                dve.wait_ge(s_ident, 4)
                for t in range(T0):
                    blk = A0[:, 0, t * PER:(t + 1) * PER, :]
                    last = nc.vector.tensor_tensor(blk, blk, ident[:].rearrange("p (b j) -> p b j", j=PAD), ALU.add)
                step(last)
                for g in range(1, NG):
                    for first, size in GROUP_RUNS[g]:
                        last = nc.vector.tensor_copy(A0[:, g, :, first:first + size], A0[:, 0, :, first:first + size])
                step(last)
                A_rows = A0[:].rearrange("p g (t b) j -> p (g t) (b j)", b=PER)
                step(nc.vector.tensor_reduce(deg[:], A_rows, AX.X, ALU.add))
                step(nc.vector.tensor_scalar(deg0[:], deg[:], 0.0, None, ALU.is_equal))
                nc.vector.tensor_tensor(dinv[:], deg[:], deg0[:], ALU.add).then_inc(s_deg, 1)
                dve.wait_ge(s_pow, 1)
                step(nc.vector.tensor_scalar(deg0[:], deg0[:], -1.0, 1.0, ALU.mult, ALU.add))
                step(nc.vector.tensor_tensor(dinv[:], dtmp[:], deg0[:], ALU.mult))
                scale = dinv[:].rearrange("p (n a) -> p n a", a=1).to_broadcast([P, NG * T0, P])
                nc.vector.tensor_tensor(A_rows, A_rows, scale, ALU.mult).then_inc(s_deg, 1)

                dve.wait_ge(s_wload, 16 * w_loads)
                for f, hi, lo in ((W12_f, W12_hi, W12_lo), (W13_f, W13_hi, W13_lo)):
                    step(nc.vector.tensor_copy(hi[:], f[:]))
                    nc.vector.tensor_tensor(lo[:], f[:], hi[:].bitcast(F32), ALU.subtract)
                step(nc.vector.tensor_scalar(one_eps2[:], eps_col[:, 0:1], 1.0, None, ALU.add))
                step(nc.vector.tensor_scalar(cI2[:], ident[:], one_eps2[:], None, ALU.mult))
                step(nc.vector.tensor_copy(cI2_hi[:], cI2[:]))
                nc.vector.tensor_tensor(cI2_lo[:], cI2[:], cI2_hi[:].bitcast(F32), ALU.subtract)
                nc.vector.tensor_scalar(cI3[:], ident[:], eps_col[:, 1:2], None, ALU.mult)

                n = [0]

                def bank():
                    dve.wait_ge(s_mm, n[0] + 1)
                    n[0] += 1
                    return banks[(n[0] - 1) % 6]

                src = bank()
                step(nc.vector.tensor_copy(WT_hi[:].rearrange("p t n -> p (t n)"), src[:]))
                nc.vector.tensor_tensor(WT_lo[:].rearrange("p t n -> p (t n)"), src[:],
                                        WT_hi[:].rearrange("p t n -> p (t n)").bitcast(F32),
                                        ALU.subtract).then_inc(s_ev, 1)
                src = bank()
                nc.vector.tensor_copy(v_rows[:].rearrange("p a n -> p (a n)"), src[:]).then_inc(s_ev, 1)
                src = bank()
                nc.vector.tensor_tensor(c_cols[:], src[:, 0:2], ba[:], ALU.add).then_inc(s_ev, 1)
                dve.wait_ge(s_fus, 1)
                step(nc.vector.reciprocal(fus_r[:], fus_s[:]))
                step(nc.vector.tensor_scalar(fus_e[:], fus_e[:], fus_r[:], None, ALU.mult))
                src = bank()
                nc.vector.tensor_tensor(mw[:], src[:, 0:NG], fus_e[:], ALU.mult).then_inc(s_ev, 1)
                for g in range(NG):
                    src = bank()
                    other = dinv[:, g * T0:(g + 1) * T0].rearrange("p (t a) -> p t a", a=1).to_broadcast([P, T0, P])
                    nc.vector.tensor_tensor(AT[:, g], src[:].rearrange("p (t n) -> p t n", n=P), other,
                                            ALU.mult).then_inc(s_ev, 1)
                for g in range(NG):
                    for d in range(DT):
                        src = bank()
                        nc.vector.tensor_copy(XaT[g][:, d, :], src[:, 0:GRAPHS * group_size(g)]).then_inc(s_ev, 1)
                dve.wait_ge(s_gload, 48)
                i = 0
                for g in range(NG):
                    for t in range(T0):
                        src = bank()
                        nc.vector.tensor_copy(Z[:, g % 2, t, :], src[:, 0:D]).then_inc(s_ev, 1)
                    for t in range(T0):
                        src = bank()
                        if i >= 2:
                            dve.wait_ge(s_or, i - 1)
                        nc.vector.tensor_tensor(Ot[:, i % 2, :], src[:, 0:D], g_b2[:, g, :], ALU.add)\
                            .then_inc(s_ev, 1)
                        i += 1

            @block.tensor
            def _(pe):
                n = [0]

                def bank():
                    if n[0] >= 6:
                        pe.wait_ge(s_ev, n[0] - 5)
                    n[0] += 1
                    return banks[(n[0] - 1) % 6]

                pe.wait_ge(s_ident, 4)
                pe.wait_ge(s_wload, 16 * w_loads)
                pe.wait_ge(s_cload, 16 * c_loads)
                dst = bank()
                for i in range(DT):
                    for o in range(DT):
                        last = nc.tensor.transpose(dst[:, i * D + o * P:i * D + (o + 1) * P],
                                                   W_nat[:, o, i * P:(i + 1) * P], ident[:])
                last.then_inc(s_mm, 1)
                dst = bank()
                for a in range(2):
                    for o in range(DT):
                        last = nc.tensor.matmul(dst[:, a * D:(a + 1) * D], wa_cols[:, a, o:o + 1].to_broadcast([P, P]),
                                                W_nat[:, o, :], start=(o == 0), stop=(o == DT - 1))
                last.then_inc(s_mm, 1)
                dst = bank()
                for a in range(2):
                    for o in range(DT):
                        last = nc.tensor.matmul(dst[:, a:a + 1], wa_cols[:, a, o:o + 1].to_broadcast([P, P]),
                                                bW_col[:, o:o + 1], start=(o == 0), stop=(o == DT - 1))
                last.then_inc(s_mm, 1)
                pe.wait_ge(s_mask, 1)
                dst = bank()
                for g in range(NG):
                    last = nc.tensor.matmul(dst[:, g:g + 1], row_mask[:, g].rearrange("p b j -> p (b j)"),
                                            ones[0:1, 0:1], start=True, stop=True)
                last.then_inc(s_mm, 1)
                pe.wait_ge(s_deg, 2)
                for g in range(NG):
                    dst = bank()
                    for t in range(T0):
                        last = nc.tensor.transpose(dst[:, t * P:(t + 1) * P],
                                                   A0[:, g, t * PER:(t + 1) * PER, :].rearrange("p b j -> p (b j)"),
                                                   ident[:])
                    last.then_inc(s_mm, 1)
                for g in range(NG):
                    size = group_size(g)
                    for d in range(DT):
                        dst = bank()
                        if d == 0:
                            pe.wait_ge(s_ev, 4 + g + 1)
                        for t in range(T0):
                            at = 0
                            for first, run in GROUP_RUNS[g]:
                                cols = dst[:, 0:GRAPHS * size].rearrange("p (b j) -> p b j", b=GRAPHS)
                                last = nc.tensor.matmul(
                                    cols[:, t * PER:(t + 1) * PER, at:at + run], X0[:, t, d * P:(d + 1) * P],
                                    AT[:, g, t, :].rearrange("p (b j) -> p b j", j=PAD)[:, :, first:first + run],
                                    start=True, stop=True)
                                at += run
                        last.then_inc(s_mm, 1)
                pe.wait_ge(s_gload, 48)
                h = 0

                def hidden(g, h):
                    size = GRAPHS * group_size(g)
                    pe.wait_ge(s_ev, 4 + NG + DT * (g + 1))
                    for m in range(KH):
                        if h >= 2:
                            pe.wait_ge(s_hev, h - 1)
                        for d in range(DT):
                            last = nc.tensor.matmul(banks[6 + h % 2][:, 0:size], G1[:, g, d, m * P:(m + 1) * P],
                                                    XaT[g][:, d, :], start=(d == 0), stop=(d == DT - 1))
                        last.then_inc(s_hmm, 1)
                        h += 1
                    return h

                h = hidden(0, h)
                for g in range(NG):
                    if g + 1 < NG:
                        h = hidden(g + 1, h)
                    pe.wait_ge(s_hev, KH * (g + 1))
                    for t in range(T0):
                        dst = bank()
                        for m in range(KH):
                            rows = H1[:, g % 2, m, t * PER:(t + 1) * PER, :].rearrange("p b j -> p (b j)")
                            last = nc.tensor.matmul(dst[:, 0:D], rows, G2[:, g, m, :], start=(m == 0), stop=(m == KH - 1))
                        last.then_inc(s_mm, 1)
                    pe.wait_ge(s_ev, n[0])
                    for t in range(T0):
                        dst = bank()
                        nc.tensor.matmul(dst[:, 0:D], AT[:, g, t, :], Z[:, g % 2, t, :],
                                         start=True, stop=True).then_inc(s_mm, 1)


def layers(nc, sb, sem, banks, ident, ones, WT_hi, WT_lo, W12_hi, W12_lo, W13_hi, W13_lo,
           W22, W23, b12, b13, rms_col, bW_row, b22_row, b23_row, v_rows, c_cols,
           cI2_hi, cI2_lo, cI3, neg_half, x, adj, x_l0, out):
    att = sb("att", [P, NT, NODES])
    adj_col = sb("adj_col", [P, 2, NT, P])
    mt_hi, mt_lo = sb("mt_hi", [P, NT, NODES], F32R), sb("mt_lo", [P, NT, NODES], F32R)
    x_res = sb("x_res", [P, NT, D])
    x_hi, x_lo = sb("x_hi", [P, NT, D], F32R), sb("x_lo", [P, NT, D], F32R)
    a_hi, a_lo = sb("a_hi", [P, DT, HALF], F32R), sb("a_lo", [P, DT, HALF], F32R)
    hid = sb("hid", [P, 2, HT3, QUARTER])
    sq = sb("sq", [P, 2, QUARTER])
    sq_sum = sb("sq_sum", [P, 2, QUARTER])
    aj_row, aj_row2 = sb("aj_row", [P, NODES]), sb("aj_row2", [P, NODES])
    neg_mask = sb("neg_mask", [P, 2, NODES], BF16)
    x_raw = sb("x_raw", [P, 2, D])
    prod = sb("prod", [P, D])
    bias_tmp = sb("bias_tmp", [P, D])
    stat = sb("stat", [P, 2, 6])
    mv = sb("mv", [P, NT, 2])
    ve, rstd = sb("ve", [P, NT]), sb("rstd", [P, NT])
    stat0 = sb("stat0", [P, 2, 6])
    mv0, ve0, rstd0 = sb("mv0", [P, NT, 2]), sb("ve0", [P, NT]), sb("rstd0", [P, NT])
    qi, qj = sb("qi", [P, NT]), sb("qj", [P, NT])
    ai, aj = sb("ai", [P, NT]), sb("aj", [P, NT])
    shift, floor = sb("shift", [P, NT]), sb("floor", [P, NT])
    top, neg_top = sb("top", [P, NT]), sb("neg_top", [P, NT])
    total, sink, sink_arg = sb("total", [P, NT]), sb("sink", [P, NT]), sb("sink_arg", [P, NT])
    den, rden, covered = sb("den", [P, NT]), sb("rden", [P, NT]), sb("covered", [P, NT])
    held, held_pool = sb("held", [P, 8]), sb("held_pool", [P, 2 * NT])
    ms, rms = sb("ms", [P, 2, 2]), sb("rms", [P, 2, 2])

    agg_bank = [[banks[0], banks[2]], [banks[1], banks[3]]]
    hid_bank = [banks[0], banks[1]]
    turn_bank = [banks[4], banks[5]]
    out_bank = [banks[6], banks[7]]

    s_att_in = [sem(f"adj_rows_loaded{t}") for t in range(NT)]
    s_col_in = [sem(f"adj_cols_loaded{i}") for i in range(2)]
    s_x_in = [sem(f"x_loaded{t}") for t in range(NT)]
    s_raw_in = [sem(f"x_raw_loaded{i}") for i in range(2)]
    s_stored = [sem(f"out_stored{t}") for t in range(NT)]
    s_turned = [sem(f"turn_bank_written{i}") for i in range(2)]
    s_turn_hi = [sem(f"turn_bank_hi_taken{i}") for i in range(2)]
    s_turn_free = [sem(f"turn_bank_lo_taken{i}") for i in range(2)]
    s_agg = [None] + [sem(f"agg_steps_l{n}") for n in (1, 2, 3)]
    s_agg_h0 = sem("agg_first_half")
    s_a_hi, s_a_lo = sem("a_hi_ready"), sem("a_lo_ready")
    s_hid_mm, s_hid_act = sem("hidden_bank_written"), sem("hidden_bank_read")
    s_sq_sum, s_rms = sem("squares_added"), sem("rms_factor")
    s_scaled, s_silu = sem("hidden_scaled"), sem("hidden_silu")
    s_out_mm, s_out_read = sem("out_bank_written"), sem("out_bank_read")
    s_var, s_rstd, s_y = sem("variance"), sem("rstd"), sem("normed")
    s_x_hi, s_x_lo, s_bias = sem("x_hi"), sem("x_lo"), sem("bias_added")
    s_diag = sem("diagonal_added")
    s_raw_used, s_var0, s_rstd0 = sem("x_raw_used"), sem("variance0"), sem("rstd0")
    s_aj, s_mask, s_mask_used = sem("aj_columns"), sem("neg_mask"), sem("neg_mask_used")
    s_top, s_exp, s_sink_arg, s_sink, s_den = sem("row_tops"), sem("exps"), sem("sink_arg"), sem("sink"), sem("denominators")
    s_dve = sem("vector_steps")

    LN = NT
    TURNS = 2 * NT + 1 + NQ
    TURN_AJ, TURN_ADJ, TURN_RMS = NT, NT + 1, 2 * NT + 1
    AGG = NT - 1
    HID = NQ * (HT2 + HT3)
    STEPS_FIRST = 3 * NT + 5 + NT + 2
    STEPS = STEPS_FIRST + 3 * 2 * NT

    def steps_by(k):
        return min(k + 1, AGG)

    def turn(b, last, u):
        return 1 + b * TURNS + u - (1 if last and u > TURN_AJ else 0)

    def split_count(b, last, u):
        return 1 + b * TURN_RMS + u - (1 if last and u > TURN_AJ else 0)

    with nc.Block() as block:
        @block.sync
        def _(sp):
            def load_x(dst, b, t, done):
                if t == 0:
                    sp.dma_start(dst[0:L0_NODES], x_l0[b]).then_inc(done, 16)
                    sp.dma_start(dst[L0_NODES:P], x[b, L0_NODES:P, :]).then_inc(done, 16)
                else:
                    sp.dma_start(dst, x[b, t * P:(t + 1) * P, :]).then_inc(done, 16)

            def load_raw(b, prior=True):
                for t in range(NT):
                    if t >= 2:
                        sp.wait_ge(s_raw_used, b * NT + t - 1)
                    elif prior:
                        sp.wait_ge(s_raw_used, b * NT)
                    load_x(x_raw[:, t % 2, :], b, t, s_raw_in[t % 2])

            def load_rows(b):
                for t in range(NT):
                    sp.dma_start(att[:, t, :], adj[b, t * P:(t + 1) * P, :]).then_inc(s_att_in[t], 16)

            def load_col(b, k):
                sp.dma_start(adj_col[:, k % 2], adj[b, :, k * P:(k + 1) * P].rearrange("(t p) m -> p t m", p=P))\
                  .then_inc(s_col_in[k % 2], 16)

            def graph(b, last):
                load_col(b, 0)
                load_col(b, 1)
                if not last:
                    load_raw(b + 1)
                    sp.wait_ge(s_turned[1], turn(b, last, NT))
                    load_rows(b + 1)
                for k in range(2, NT):
                    sp.wait_ge(s_turned[1], turn(b, last, TURN_ADJ + k - 1))
                    load_col(b, k)
                for t in range(NT):
                    sp.wait_ge(s_y, b * 4 * LN + 3 * LN + t + 1)
                    sp.dma_start(out[b, t * P:(t + 1) * P, :], x_res[:, t, :]).then_inc(s_stored[t], 16)
                    if t >= 2 and not last:
                        next_x(b, t - 2)
                if not last:
                    next_x(b, NT - 2)
                    next_x(b, NT - 1)

            def next_x(b, t):
                sp.wait_ge(s_stored[t], (b + 1) * 16)
                load_x(x_res[:, t, :], b + 1, t, s_x_in[t])

            load_raw(0, prior=False)
            load_rows(0)
            for t in range(NT):
                load_x(x_res[:, t, :], 0, t, s_x_in[t])
            with sp.Fori(0, GRAPHS - 1) as b:
                graph(b, False)
            graph(GRAPHS - 1, True)
            for t in range(NT):
                sp.wait_ge(s_stored[t], GRAPHS * 16)

        @block.tensor
        def _(pe):
            def turn_begin(i, b, last, u):
                if i == 0:
                    pe.wait_ge(s_turn_free[0], turn(b, last, u))
                else:
                    pe.wait_ge(s_turn_free[1], split_count(b, last, min(u, TURN_RMS)))
                    if u > TURN_RMS:
                        pe.wait_ge(s_scaled, b * NQ * HT3 + (u - TURN_RMS) * HT3)

            def turn_att(b, last, k):
                for i in range(2):
                    turn_begin(i, b, last, k)
                    for j in range(4):
                        mm = nc.tensor.transpose(turn_bank[i][:, j * P:(j + 1) * P],
                                                 att[:, 4 * i + j, k * P:(k + 1) * P], ident[:])
                    mm.then_inc(s_turned[i], 1)

            def turn_col(b, last, k):
                pe.wait_ge(s_diag, b * NT + k + 1)
                for i in range(2):
                    turn_begin(i, b, last, TURN_ADJ + k)
                    for j in range(4):
                        mm = nc.tensor.transpose(turn_bank[i][:, j * P:(j + 1) * P],
                                                 adj_col[:, k % 2, 4 * i + j, :], ident[:])
                    mm.then_inc(s_turned[i], 1)

            def aj_rows(aj_count, begin):
                pe.wait_ge(s_aj, aj_count)
                for i in range(2):
                    begin(i)
                    for j in range(4):
                        t = 4 * i + j
                        mm = nc.tensor.matmul(turn_bank[i][:, j * P:(j + 1) * P], aj[:, t:t + 1].to_broadcast([P, P]),
                                              ident[:], start=True, stop=True)
                    mm.then_inc(s_turned[i], 1)

            def agg_step(layer, k, h, first, last_k):
                for d in range(DT):
                    dst = agg_bank[d][h]
                    cols = slice(h * HALF, (h + 1) * HALF)
                    hi, lo = x_hi[:, k, d * P:(d + 1) * P], x_lo[:, k, d * P:(d + 1) * P]
                    extra = layer == 2 and k // 4 == h
                    nc.tensor.matmul(dst[:], hi, mt_hi[:, k, cols], start=first, stop=False)
                    nc.tensor.matmul(dst[:], hi, mt_lo[:, k, cols], start=False, stop=False)
                    mm = nc.tensor.matmul(dst[:], lo, mt_hi[:, k, cols], start=False, stop=last_k and not extra,
                                          skip_group_check=False)
                    if extra:
                        own = dst[:, (k % 4) * P:(k % 4 + 1) * P]
                        nc.tensor.matmul(own, hi, cI2_hi[:], start=False, stop=False)
                        nc.tensor.matmul(own, hi, cI2_lo[:], start=False, stop=False)
                        mm = nc.tensor.matmul(own, lo, cI2_hi[:], start=False, stop=last_k)
                return mm

            def aggregate(b, last, layer):
                turned = {1: turn_att, 2: turn_col}.get(layer)
                use = {1: 0, 2: TURN_ADJ}.get(layer)
                for k in range(NT):
                    if turned and k + 2 < NT:
                        turned(b, last, k + 2)
                    if turned:
                        pe.wait_ge(s_turn_free[0], turn(b, last, use + k + 1))
                        pe.wait_ge(s_turn_free[1], split_count(b, last, use + k + 1))
                    pe.wait_ge(s_x_lo, b * 3 * LN + (layer - 1) * LN + k + 1)
                    if k < NT - 2:
                        agg_step(layer, k, 0, k == 0, False)
                        agg_step(layer, k, 1, k == 0, False).then_inc(s_agg[layer], 1)
                agg_step(layer, NT - 2, 0, False, False)
                agg_step(layer, NT - 1, 0, False, True).then_inc(s_agg_h0, 1)
                agg_step(layer, NT - 2, 1, False, False)
                agg_step(layer, NT - 1, 1, False, True).then_inc(s_agg[layer], 1)

            def split_product(dst, a_cols, w_hi, w_lo, w_cols, hidden):
                for d in range(DT):
                    ah, al = a_hi[:, d, a_cols], a_lo[:, d, a_cols]
                    wh, wl = w_hi[:, d, w_cols], w_lo[:, d, w_cols]
                    for n, (l, r) in enumerate(((wh, ah), (wh, al), (wl, ah)) if hidden else ((ah, wh), (ah, wl), (al, wh))):
                        mm = nc.tensor.matmul(dst, l, r, start=(d == 0 and n == 0), stop=(d == DT - 1 and n == 2))
                return mm

            def a_ready(b, layer, h):
                pe.wait_ge(s_a_lo, b * 6 * DT + ((layer - 1) * 2 + h + 1) * DT)

            def out_free(b, i):
                if i >= 2:
                    pe.wait_ge(s_out_read, b * 3 * LN + i - 1)

            def attention_out(b, t):
                out_free(b, t)
                mm = split_product(out_bank[t % 2][:, 0:D], slice((t % 4) * P, (t % 4 + 1) * P),
                                   WT_hi, WT_lo, slice(0, D), False)
                mm.then_inc(s_out_mm, 1)

            def hidden_tile(b, layer, q, m):
                i = (0 if layer == 2 else NQ * HT2) + q * (HT2 if layer == 2 else HT3) + m
                if i >= 2:
                    pe.wait_ge(s_hid_act, b * HID + i - 1)
                w_hi, w_lo = (W12_hi, W12_lo) if layer == 2 else (W13_hi, W13_lo)
                mm = split_product(hid_bank[i % 2][:, 0:QUARTER], slice((q % 2) * QUARTER, (q % 2 + 1) * QUARTER),
                                   w_hi, w_lo, slice(m * P, (m + 1) * P), True)
                mm.then_inc(s_hid_mm, 1)

            def second_product(b, layer, q, between=None):
                W2, tiles = (W22, HT2) if layer == 2 else (W23, HT3)
                for j in range(2):
                    out_free(b, (layer - 1) * NT + 2 * q + j)
                for m in range(tiles):
                    if layer == 2:
                        pe.wait_ge(s_hid_act, b * HID + q * HT2 + m + 1)
                    else:
                        pe.wait_ge(s_silu, b * NQ * HT3 + q * HT3 + m + 1)
                    for j in range(2):
                        mm = nc.tensor.matmul(out_bank[j][:, 0:D], hid[:, q % 2, m, j * P:(j + 1) * P], W2[:, m, :],
                                              start=(m == 0), stop=(m == tiles - 1))
                        if m == tiles - 1:
                            mm.then_inc(s_out_mm, 1)
                    if between and m in between:
                        between[m]()

            def rms_sum(b, last, q):
                pe.wait_ge(s_sq_sum, b * NQ * (HT3 - 1) + (q + 1) * (HT3 - 1))
                turn_begin(0, b, last, TURN_RMS + q)
                for j in range(2):
                    mm = nc.tensor.matmul(turn_bank[0][:, j:j + 1], sq_sum[:, q % 2, j * P:(j + 1) * P], ones[:, 0:1],
                                          start=True, stop=True)
                mm.then_inc(s_turned[0], 1)

            def rms_row(b, last, q):
                pe.wait_ge(s_rms, b * NQ + q + 1)
                turn_begin(1, b, last, TURN_RMS + q)
                for j in range(2):
                    mm = nc.tensor.matmul(turn_bank[1][:, j * P:(j + 1) * P],
                                          rms[:, q % 2, j:j + 1].to_broadcast([P, P]), ident[:], start=True, stop=True)
                mm.then_inc(s_turned[1], 1)

            def graph(b, last):
                pe.wait_ge(s_exp, (b + 1) * NT)
                turn_att(b, last, 0)
                turn_att(b, last, 1)
                aggregate(b, last, 1)
                if not last:
                    aj_rows(b + 2, lambda i: turn_begin(i, b, last, TURN_AJ))
                turn_col(b, last, 0)
                a_ready(b, 1, 0)
                for t in range(NT // 2):
                    attention_out(b, t)
                turn_col(b, last, 1)
                a_ready(b, 1, 1)
                for t in range(NT // 2, NT):
                    attention_out(b, t)
                aggregate(b, last, 2)
                a_ready(b, 2, 0)
                for q in range(NQ):
                    if q == 2:
                        a_ready(b, 2, 1)
                    for m in range(HT2):
                        hidden_tile(b, 2, q, m)
                    if q >= 1:
                        second_product(b, 2, q - 1)
                second_product(b, 2, NQ - 1)
                aggregate(b, last, 3)
                a_ready(b, 3, 0)
                for q in range(NQ):
                    if q == 2:
                        a_ready(b, 3, 1)
                    for m in range(HT3):
                        hidden_tile(b, 3, q, m)
                        if q >= 1 and m == 2:
                            rms_sum(b, last, q - 1)
                        if q >= 1 and m == 4:
                            rms_row(b, last, q - 1)
                    if q == NQ - 1:
                        second_product(b, 3, q - 1, {2: lambda: rms_sum(b, last, NQ - 1),
                                                     6: lambda: rms_row(b, last, NQ - 1)})
                    elif q >= 1:
                        second_product(b, 3, q - 1)
                second_product(b, 3, NQ - 1)

            pe.sem_inc(s_agg[3], AGG)
            aj_rows(1, lambda i: None)
            with pe.Fori(0, GRAPHS - 1) as b:
                graph(b, False)
            graph(GRAPHS - 1, True)

        @block.scalar
        def _(act):
            def turn_hi(b, last, use, k):
                for i in range(2):
                    act.wait_ge(s_turned[i], turn(b, last, use + k + 1))
                    nc.scalar.activation(mt_hi[:, k, i * HALF:(i + 1) * HALF], turn_bank[i][:], ACT.Copy)\
                      .then_inc(s_turn_hi[i], 1)

            def take_att(b, last, k):
                act.wait_ge(s_agg[3], b * AGG + steps_by(k))
                turn_hi(b, last, 0, k)

            def take_col(b, last, k):
                act.wait_ge(s_agg[1], b * AGG + steps_by(k))
                turn_hi(b, last, TURN_ADJ, k)

            def aj_copy(count):
                for i in range(2):
                    act.wait_ge(s_turned[i], count + 1)
                    nc.scalar.activation(aj_row[:, i * HALF:(i + 1) * HALF], turn_bank[i][:], ACT.Copy)\
                      .then_inc(s_turn_hi[i], 1)

            def agg_hi(b, layer, h):
                if h == 0:
                    act.wait_ge(s_agg_h0, b * 3 + layer)
                else:
                    act.wait_ge(s_agg[layer], (b + (1 if layer == 3 else 0)) * AGG + AGG)
                if h == 1:
                    used, count = {1: (s_out_mm, b * 3 * NT + NT // 2),
                                   2: (s_hid_mm, b * HID + NQ // 2 * HT2),
                                   3: (s_hid_mm, b * HID + NQ * HT2 + NQ // 2 * HT3)}[layer]
                    act.wait_ge(used, count)
                for d in range(DT):
                    nc.scalar.activation(a_hi[:, d, :], agg_bank[d][h][:], ACT.Copy).then_inc(s_a_hi, 1)

            def x_high(b, norm, t):
                act.wait_ge(s_y, b * 4 * LN + norm * LN + t + 1)
                nc.scalar.activation(x_hi[:, t, :], x_res[:, t, :], ACT.Copy).then_inc(s_x_hi, 1)

            def exp(b, t):
                act.wait_ge(s_top, b * NT + t + 1)
                nc.scalar.activation(att[:, t, :], att[:, t, :], ACT.Exp, bias=neg_top[:, t:t + 1],
                                     accum_out=total[:, t:t + 1]).then_inc(s_exp, 1)

            def sink_exp(b):
                act.wait_ge(s_sink_arg, b + 1)
                nc.scalar.activation(sink[:], sink_arg[:], ACT.Exp).then_inc(s_sink, 1)

            def relu(b, q):
                for m in range(HT2):
                    i = q * HT2 + m
                    act.wait_ge(s_hid_mm, b * HID + i + 1)
                    nc.scalar.activation(hid[:, q % 2, m, :], hid_bank[i % 2][:, 0:QUARTER], ACT.Relu,
                                         bias=b12[:, m:m + 1]).then_inc(s_hid_act, 1)

            def hidden_and_square(b, last, q, m):
                i = NQ * HT2 + q * HT3 + m
                src = hid_bank[i % 2][:, 0:QUARTER]
                act.wait_ge(s_hid_mm, b * HID + i + 1)
                nc.scalar.activation(hid[:, q % 2, m, :], src, ACT.Identity, bias=b13[:, m:m + 1])
                n = q * (HT3 - 1) + m
                if m == 0:
                    dst = sq_sum[:, q % 2, :]
                else:
                    if m >= 3:
                        act.wait_ge(s_sq_sum, b * NQ * (HT3 - 1) + n - 2)
                    elif q >= 1:
                        act.wait_ge(s_sq_sum, b * NQ * (HT3 - 1) + q * (HT3 - 1))
                    dst = sq[:, m % 2, :]
                nc.scalar.activation(dst, src, ACT.Square, bias=b13[:, m:m + 1])\
                  .then_inc(s_hid_act, 1)

            def silu(b, q, m):
                act.wait_ge(s_scaled, b * NQ * HT3 + q * HT3 + m + 1)
                nc.scalar.activation(hid[:, q % 2, m, :], hid[:, q % 2, m, :], ACT.Silu).then_inc(s_silu, 1)

            def graph(b, last):
                x_high(b, 0, 0)
                x_high(b, 0, 1)
                for k in range(NT):
                    take_att(b, last, k)
                    if k + 2 < NT:
                        x_high(b, 0, k + 2)
                agg_hi(b, 1, 0)
                if not last:
                    aj_copy(turn(b, last, TURN_AJ))
                take_col(b, last, 0)
                agg_hi(b, 1, 1)
                take_col(b, last, 1)
                for k in range(2, NT):
                    x_high(b, 1, k - 2)
                    take_col(b, last, k)
                x_high(b, 1, NT - 2)
                x_high(b, 1, NT - 1)
                agg_hi(b, 2, 0)
                relu(b, 0)
                relu(b, 1)
                agg_hi(b, 2, 1)
                if not last:
                    exp(b + 1, 0)
                relu(b, 2)
                x_high(b, 2, 0)
                x_high(b, 2, 1)
                if not last:
                    exp(b + 1, 1)
                relu(b, 3)
                x_high(b, 2, 2)
                x_high(b, 2, 3)
                if not last:
                    exp(b + 1, 2)
                x_high(b, 2, 4)
                x_high(b, 2, 5)
                if not last:
                    exp(b + 1, 3)
                x_high(b, 2, 6)
                x_high(b, 2, 7)
                if not last:
                    for t in range(4, NT):
                        exp(b + 1, t)
                    sink_exp(b + 1)
                agg_hi(b, 3, 0)
                for q in range(NQ):
                    for m in range(HT3):
                        hidden_and_square(b, last, q, m)
                        if q >= 1 and m >= 5:
                            silu(b, q - 1, m - 5)
                    if q == 1:
                        agg_hi(b, 3, 1)
                    if q >= 1:
                        for m in range(3, HT3):
                            silu(b, q - 1, m)
                for m in range(HT3):
                    silu(b, NQ - 1, m)

            aj_copy(0)
            for t in range(NT):
                exp(0, t)
            sink_exp(0)
            with act.Fori(0, GRAPHS - 1) as b:
                graph(b, False)
            graph(GRAPHS - 1, True)

        @block.gpsimd
        def _(pool):
            def hold(place):
                nc.gpsimd.tensor_tensor(held_pool[:, place:place + 1], ones[:, 0:1], ones[:, 1:2], ALU.add)

            def rstd_of(b, norm, t):
                pool.wait_ge(s_var, b * 3 * LN + (norm - 1) * LN + t + 1)
                nc.gpsimd.tensor_tensor(rstd[:, t:t + 1], ve[:, t:t + 1], neg_half[:, 0:1], ALU.pow).then_inc(s_rstd, 1)

            def x_low(b, norm, t):
                pool.wait_ge(s_x_hi, b * 3 * LN + norm * LN + t + 1)
                nc.gpsimd.tensor_tensor(x_lo[:, t, :], x_res[:, t, :], x_hi[:, t, :].bitcast(F32),
                                        ALU.subtract).then_inc(s_x_lo, 1)
                if norm == 0:
                    if t == 0:
                        pool.wait_ge(s_den, b + 1)
                    if t >= 1:
                        pool.wait_ge(s_bias, b * 4 * LN + 2 * t)
                    hold(NT + t)
                    nc.gpsimd.tensor_scalar(bias_tmp[:], bW_row[:], covered[:, t:t + 1], None, ALU.mult)\
                      .then_inc(s_bias, 1)
                    bias = bias_tmp[:]
                    pool.wait_ge(s_bias, b * 4 * LN + 2 * t + 1)
                else:
                    bias = (b22_row if norm == 1 else b23_row)[:]
                nc.gpsimd.tensor_tensor(x_res[:, t, :], x_res[:, t, :], bias, ALU.add).then_inc(s_bias, 1)

            def diagonal(b, k):
                pool.wait_ge(s_col_in[k % 2], b * 16 * (NT // 2) + 16 * (k // 2 + 1))
                own = adj_col[:, k % 2, k, :]
                nc.gpsimd.tensor_tensor(own, own, cI3[:], ALU.add).then_inc(s_diag, 1)

            def masks(b, t, prior=True):
                pool.wait_ge(s_att_in[t], (b + 1) * 16)
                if t >= 2:
                    pool.wait_ge(s_mask_used, b * NT + t - 1)
                elif prior:
                    pool.wait_ge(s_mask_used, b * NT)
                hold(t)
                nc.gpsimd.tensor_scalar(neg_mask[:, t % 2, :], att[:, t, :], 0.0, MASKED, ALU.is_le, ALU.mult)\
                  .then_inc(s_mask, 1)

            def rstd0_of(b):
                pool.wait_ge(s_var0, b + 1)
                nc.gpsimd.tensor_tensor(rstd0[:], ve0[:], neg_half[:, 0:NT], ALU.pow).then_inc(s_rstd0, 1)

            def add_square(b, q, m):
                pool.wait_ge(s_hid_act, b * HID + NQ * HT2 + q * HT3 + m + 1)
                if m >= 2:
                    pool.wait_ge(s_sq_sum, b * NQ * (HT3 - 1) + q * (HT3 - 1) + m - 1)
                total_sq = sq_sum[:, q % 2, :]
                nc.gpsimd.tensor_tensor(total_sq, total_sq, sq[:, m % 2, :], ALU.add).then_inc(s_sq_sum, 1)

            def rms_of(b, last, q):
                pool.wait_ge(s_turn_free[0], turn(b, last, TURN_RMS + q + 1))
                nc.gpsimd.tensor_tensor(rms[:, q % 2, :], ms[:, q % 2, :], neg_half[:, 0:2], ALU.pow).then_inc(s_rms, 1)

            def graph(b, last):
                for t in range(NT):
                    x_low(b, 0, t)
                diagonal(b, 0)
                diagonal(b, 1)
                if not last:
                    rstd0_of(b + 1)
                rstd_of(b, 1, 0)
                for t in range(NT):
                    if t + 1 < NT:
                        rstd_of(b, 1, t + 1)
                    x_low(b, 1, t)
                    if t + 2 < NT:
                        diagonal(b, t + 2)
                if not last:
                    masks(b + 1, 0)
                    masks(b + 1, 1)
                for q in range(NQ):
                    rstd_of(b, 2, 2 * q)
                    rstd_of(b, 2, 2 * q + 1)
                    x_low(b, 2, 2 * q)
                    x_low(b, 2, 2 * q + 1)
                    if not last and q < 2:
                        masks(b + 1, q + 2)
                if not last:
                    for t in range(4, NT):
                        masks(b + 1, t)
                for q in range(NQ):
                    for m in range(1, HT3):
                        add_square(b, q, m)
                        if q >= 1 and m == 2:
                            rms_of(b, last, q - 1)
                            if q >= 2:
                                rstd_of(b, 3, 2 * q - 4)
                                rstd_of(b, 3, 2 * q - 3)
                rms_of(b, last, NQ - 1)
                for t in range(NT - 4, NT):
                    rstd_of(b, 3, t)

            rstd0_of(0)
            for t in range(NT):
                masks(0, t, prior=False)
            with pool.Fori(0, GRAPHS - 1) as b:
                graph(b, False)
            graph(GRAPHS - 1, True)

        @block.vector
        def _(dve):
            taken = [0]

            def step(base, ins):
                taken[0] += 1
                ins.then_inc(s_dve, 1)
                dve.wait_ge(s_dve, base + taken[0])

            holds = [0]

            def hold():
                holds[0] = (holds[0] + 1) % 8
                nc.vector.tensor_copy(held[:, holds[0]:holds[0] + 1], ones[:, 0:1])

            def turn_lo(b, last, use, k):
                for i in range(2):
                    dve.wait_ge(s_turn_hi[i], split_count(b, last, use + k + 1))
                    cols = slice(i * HALF, (i + 1) * HALF)
                    nc.vector.tensor_tensor(mt_lo[:, k, cols], turn_bank[i][:], mt_hi[:, k, cols].bitcast(F32),
                                            ALU.subtract).then_inc(s_turn_free[i], 1)

            def aj_scaled(count):
                for i in range(2):
                    dve.wait_ge(s_turn_hi[i], count + 1)
                    nc.vector.tensor_scalar(aj_row2[:, i * HALF:(i + 1) * HALF], turn_bank[i][:], SLOPE, None,
                                            ALU.mult).then_inc(s_turn_free[i], 1)

            def agg_lo(b, layer, h):
                n = ((layer - 1) * 2 + h) * DT
                for d in range(DT):
                    dve.wait_ge(s_a_hi, b * 6 * DT + n + d + 1)
                    nc.vector.tensor_tensor(a_lo[:, d, :], agg_bank[d][h][:], a_hi[:, d, :].bitcast(F32),
                                            ALU.subtract).then_inc(s_a_lo, 1)

            def residual(b, layer, t):
                i = (layer - 1) * NT + t
                dve.wait_ge(s_out_mm, b * 3 * LN + i + 1)
                dve.wait_ge(s_bias, b * 4 * LN + (2 * t + 2 if layer == 1 else layer * LN + t + 1))
                src = out_bank[i % 2][:, 0:D]
                if layer == 1:
                    ins = nc.vector.scalar_tensor_tensor(out=x_res[:, t, :], in0=src, scalar=rden[:, t:t + 1],
                                                         in1=x_res[:, t, :], op0=ALU.mult, op1=ALU.add)
                else:
                    ins = nc.vector.tensor_tensor(x_res[:, t, :], src, x_res[:, t, :], ALU.add)
                ins.then_inc(s_out_read, 1)

            def statistics(b, layer, t, base):
                dve.wait_ge(s_out_read, b * 3 * LN + (layer - 1) * NT + t + 1)
                step(base, nc.vector.bn_stats(stat[:, t % 2, :], x_res[:, t, :]))
                hold()
                step(base, nc.vector.bn_aggr(mv[:, t, :], stat[:, t % 2, :]))
                nc.vector.tensor_scalar(ve[:, t:t + 1], mv[:, t, 1:2], LN_EPS, None, ALU.add).then_inc(s_var, 1)

            def normalize(b, layer, t):
                dve.wait_ge(s_rstd, b * 3 * LN + (layer - 1) * LN + t + 1)
                nc.vector.tensor_scalar(x_res[:, t, :], x_res[:, t, :], mv[:, t, 0:1], rstd[:, t:t + 1],
                                        ALU.subtract, ALU.mult).then_inc(s_y, 1)

            def normalize0(b, t):
                dve.wait_ge(s_x_in[t], b * (32 if t == 0 else 16) + (32 if t == 0 else 16))
                nc.vector.tensor_scalar(x_res[:, t, :], x_res[:, t, :], mv0[:, t, 0:1], rstd0[:, t:t + 1],
                                        ALU.subtract, ALU.mult).then_inc(s_y, 1)

            def attention_sums(b, t, base):
                raw_counts = ((NT // 2) * 16 + 16, (NT // 2) * 16)[t % 2]
                done = 16 * (t // 2 + 1) + (16 if t % 2 == 0 else 0)
                dve.wait_ge(s_raw_in[t % 2], b * raw_counts + done)
                src = x_raw[:, t % 2, :]
                step(base, nc.vector.bn_stats(stat0[:, t % 2, :], src))
                hold()
                step(base, nc.vector.bn_aggr(mv0[:, t, :], stat0[:, t % 2, :]))
                mean = mv0[:, t, 0:1]
                step(base, nc.vector.scalar_tensor_tensor(out=prod[:], in0=src, scalar=mean, in1=v_rows[:, 0, :],
                                                          op0=ALU.subtract, op1=ALU.mult, accum_out=qi[:, t:t + 1]))
                ins = nc.vector.scalar_tensor_tensor(out=prod[:], in0=src, scalar=mean, in1=v_rows[:, 1, :],
                                                     op0=ALU.subtract, op1=ALU.mult, accum_out=qj[:, t:t + 1])
                ins.then_inc(s_raw_used, 1)

            def attention_columns(b, base):
                dve.wait_ge(s_raw_used, (b + 1) * NT)
                nc.vector.tensor_scalar(ve0[:], mv0[:, :, 1], LN_EPS, None, ALU.add).then_inc(s_var0, 1)
                dve.wait_ge(s_rstd0, b + 1)
                step(base, nc.vector.tensor_tensor(aj[:], qj[:], rstd0[:], ALU.mult))
                step(base, nc.vector.tensor_tensor(ai[:], qi[:], rstd0[:], ALU.mult))
                nc.vector.tensor_scalar(aj[:], aj[:], c_cols[:, 1:2], None, ALU.add).then_inc(s_aj, 1)
                step(base, nc.vector.tensor_scalar(ai[:], ai[:], c_cols[:, 0:1], None, ALU.add))
                step(base, nc.vector.tensor_scalar(shift[:], ai[:], SLOPE - 1.0, None, ALU.mult))
                step(base, nc.vector.tensor_scalar(floor[:], ai[:], -1.0, SINK, ALU.mult, ALU.add))

            def scores(b, t, base):
                dve.wait_ge(s_mask, b * NT + t + 1)
                step(base, nc.vector.scalar_tensor_tensor(out=att[:, t, :], in0=aj_row2[:], scalar=shift[:, t:t + 1],
                                                          in1=aj_row[:], op0=ALU.add, op1=ALU.max))
                hold()
                nc.vector.tensor_tensor_reduce(out=att[:, t, :], in0=att[:, t, :], in1=neg_mask[:, t % 2, :],
                                               scale=1.0, scalar=-3.0e38, op0=ALU.add, op1=ALU.max,
                                               accum_out=top[:, t:t + 1]).then_inc(s_mask_used, 1)
                dve.wait_ge(s_mask_used, b * NT + t + 1)
                nc.vector.tensor_scalar(neg_top[:, t:t + 1], top[:, t:t + 1], floor[:, t:t + 1], -1.0,
                                        ALU.max, ALU.mult).then_inc(s_top, 1)

            def denominators(b, base):
                dve.wait_ge(s_top, (b + 1) * NT)
                nc.vector.tensor_tensor(sink_arg[:], floor[:], neg_top[:], ALU.add).then_inc(s_sink_arg, 1)
                dve.wait_ge(s_exp, (b + 1) * NT)
                dve.wait_ge(s_sink, b + 1)
                step(base, nc.vector.tensor_tensor(den[:], total[:], sink[:], ALU.add))
                step(base, nc.vector.reciprocal(rden[:], den[:]))
                nc.vector.tensor_tensor(covered[:], total[:], rden[:], ALU.mult).then_inc(s_den, 1)

            def mean_square(b, last, q):
                dve.wait_ge(s_turned[0], turn(b, last, TURN_RMS + q + 1))
                nc.vector.tensor_scalar(ms[:, q % 2, :], turn_bank[0][:, 0:2], 1.0 / HID3, RMS_EPS, ALU.mult, ALU.add)\
                  .then_inc(s_turn_free[0], 1)

            def scale_hidden(b, last, q, m):
                if m == 0:
                    dve.wait_ge(s_turned[1], turn(b, last, TURN_RMS + q + 1))
                dve.wait_ge(s_hid_act, b * HID + NQ * HT2 + q * HT3 + m + 1)
                h = hid[:, q % 2, m, :]
                ins = nc.vector.scalar_tensor_tensor(out=h, in0=h, scalar=rms_col[:, m:m + 1],
                                                     in1=turn_bank[1][:, 0:QUARTER], op0=ALU.mult, op1=ALU.mult)
                ins.then_inc(s_scaled, 1)

            def graph(b, last, base):
                normalize0(b, 0)
                normalize0(b, 1)
                for k in range(NT):
                    turn_lo(b, last, 0, k)
                    if k + 2 < NT:
                        normalize0(b, k + 2)
                    if k >= 2 and not last:
                        attention_sums(b + 1, k - 2, base)
                agg_lo(b, 1, 0)
                if not last:
                    attention_sums(b + 1, NT - 2, base)
                    attention_sums(b + 1, NT - 1, base)
                    attention_columns(b + 1, base)
                    aj_scaled(split_count(b, last, TURN_AJ))
                turn_lo(b, last, TURN_ADJ, 0)
                for t in range(NT // 2):
                    residual(b, 1, t)
                agg_lo(b, 1, 1)
                turn_lo(b, last, TURN_ADJ, 1)
                for t in range(NT // 2, NT):
                    residual(b, 1, t)
                statistics(b, 1, 0, base)
                statistics(b, 1, 1, base)
                for t in range(NT):
                    normalize(b, 1, t)
                    if t + 2 < NT:
                        turn_lo(b, last, TURN_ADJ, t + 2)
                        statistics(b, 1, t + 2, base)
                agg_lo(b, 2, 0)
                if not last:
                    dve.wait_ge(s_turn_free[0], turn(b, last, TURN_AJ + 1))
                    dve.wait_ge(s_turn_free[1], split_count(b, last, TURN_AJ + 1))
                    scores(b + 1, 0, base)
                agg_lo(b, 2, 1)
                for q in range(NQ):
                    residual(b, 2, 2 * q)
                    residual(b, 2, 2 * q + 1)
                    statistics(b, 2, 2 * q, base)
                    statistics(b, 2, 2 * q + 1, base)
                    normalize(b, 2, 2 * q)
                    normalize(b, 2, 2 * q + 1)
                    if not last and q < NQ - 1:
                        scores(b + 1, q + 1, base)
                if not last:
                    for t in range(4, NT):
                        scores(b + 1, t, base)
                    denominators(b + 1, base)
                agg_lo(b, 3, 0)
                for q in range(NQ):
                    if q == NQ - 1:
                        mean_square(b, last, q)
                    if q >= 1:
                        residual(b, 3, 2 * q - 2)
                        residual(b, 3, 2 * q - 1)
                    if q < NQ - 1:
                        mean_square(b, last, q)
                    if q >= 1 and q < NQ - 1:
                        for t in (2 * q - 2, 2 * q - 1):
                            statistics(b, 3, t, base)
                        for t in (2 * q - 2, 2 * q - 1):
                            normalize(b, 3, t)
                    for m in range(HT3):
                        scale_hidden(b, last, q, m)
                        if q == 0 and m == 2:
                            agg_lo(b, 3, 1)
                for t in (NT - 2, NT - 1):
                    residual(b, 3, t)
                for t in range(NT - 4, NT):
                    statistics(b, 3, t, base)
                for t in range(NT - 4, NT):
                    normalize(b, 3, t)

            for t in range(NT):
                attention_sums(0, t, 0)
            attention_columns(0, 0)
            aj_scaled(0)
            for i in range(2):
                dve.wait_ge(s_turn_free[i], 1)
            for t in range(NT):
                scores(0, t, 0)
            denominators(0, 0)
            assert taken[0] == STEPS_FIRST
            with dve.Fori(0, GRAPHS - 1) as b:
                taken[0] = 0
                graph(b, False, b * STEPS + STEPS_FIRST)
                assert taken[0] == STEPS
            taken[0] = 0
            graph(GRAPHS - 1, True, (GRAPHS - 1) * STEPS + STEPS_FIRST)


_INS = ['x', 'adj', 'L0_gnn_W1', 'L0_gnn_b1', 'L0_gnn_W2', 'L0_gnn_b2', 'L0_gnn_fusion_w', 'L1_gnn_W',
        'L1_gnn_bW', 'L1_gnn_wai', 'L1_gnn_bai', 'L1_gnn_waj', 'L1_gnn_baj', 'L2_gnn_eps', 'L2_gnn_W1',
        'L2_gnn_b1', 'L2_gnn_W2', 'L2_gnn_b2', 'L3_gnn_epsilon', 'L3_gnn_W1', 'L3_gnn_b1',
        'L3_gnn_rms_weight', 'L3_gnn_W2', 'L3_gnn_b2']


def kernel(**inputs):
    import numpy as _np
    import concourse.bacc as _bacc
    from concourse import mybir as _mybir
    from concourse.bass_utils import run_bass_kernel_spmd as _run

    nc = _bacc.Bacc("TRN2", target_bir_lowering=False, num_devices=1, dynamic_dma_scratch_size=1024)
    arrays, args = {}, []
    for name in _INS:
        a = _np.ascontiguousarray(inputs[name])
        if name == 'L3_gnn_epsilon':
            a = a.reshape(1)
        arrays[f"in_{name}"] = a
        args.append(nc.dram_tensor(f"in_{name}", a.shape, _mybir.dt.from_np(a.dtype), kind="ExternalInput").ap())
    out = nc.dram_tensor("out", (GRAPHS, NODES, D), F32, kind="ExternalOutput").ap()
    adj_resnorm(nc, *args, out)
    r = _run(nc, [arrays], core_ids=[0])
    return r.results[0]["out"]
```

```python
from contextlib import ExitStack

import concourse.bass as bass
from concourse import mybir

F32 = mybir.dt.float32
F32R = mybir.dt.float32r
ALU = mybir.AluOpType
ACT = mybir.ActivationFunctionType
AX = mybir.AxisListType

P = 128
GRAPHS, NODES, D = 16, 1024, 256
NT = NODES // P
DT = D // P
HALF = 512
QUARTER = 256
NQ = NODES // QUARTER
CR = 3
HID2, HID3 = 512, 1024
HT2, HT3 = HID2 // P, HID3 // P
LN_EPS, RMS_EPS = 1e-5, 1e-6
SLOPE = 0.2
MASKED, SINK = -9.0e15, -1.0e9

L0_NODES, L0_HID = 25, 512
GROUP_RUNS = [[(0, 25)], [(0, 9)], [(0, 1), (9, 6)], [(6, 3), (12, 3)], [(3, 3), (9, 3)]]
NG = len(GROUP_RUNS)
PAD = 32
PER = P // PAD
T0 = GRAPHS // PER


def group_size(g):
    return sum(n for _, n in GROUP_RUNS[g])


def row(ap):
    return ap.rearrange("(a n) -> a n", a=1)


def adj_resnorm(nc, x, adj, L0_W1, L0_b1, L0_W2, L0_b2, L0_fusion_w, W, bW, wai, bai, waj, baj,
                eps2, L2_W1, L2_b1, L2_W2, L2_b2, eps3, L3_W1, L3_b1, rms_w, L3_W2, L3_b2, out):
    x_l0 = nc.dram_tensor("x_after_l0", (GRAPHS, L0_NODES, D), F32, kind="Internal").ap()

    with ExitStack() as ctx:
        def sb(name, shape, dt=F32, c=ctx):
            return c.enter_context(nc.sbuf_tensor(name, shape, dt))

        def sem(name):
            return ctx.enter_context(nc.semaphore(name))

        ident = sb("ident", [P, P])
        ones = sb("ones", [P, P])
        WT_hi, WT_lo = sb("WT_hi", [P, DT, D], F32R), sb("WT_lo", [P, DT, D], F32R)
        W12_hi, W12_lo = sb("W12_hi", [P, DT, HID2], F32R), sb("W12_lo", [P, DT, HID2], F32R)
        W13_hi, W13_lo = sb("W13_hi", [P, DT, HID3], F32R), sb("W13_lo", [P, DT, HID3], F32R)
        W22 = sb("W22", [P, HT2, D])
        W23 = sb("W23", [P, HT3, D])
        b12 = sb("b12", [P, HT2])
        b13 = sb("b13", [P, HT3])
        rms_col = sb("rms_col", [P, HT3])
        bW_row = sb("bW_row", [P, D])
        b22_row = sb("b22_row", [P, D])
        b23_row = sb("b23_row", [P, D])
        v_rows = sb("v_rows", [P, 2, D])
        c_cols = sb("c_cols", [P, 2])
        cI2_hi, cI2_lo = sb("cI2_hi", [P, P], F32R), sb("cI2_lo", [P, P], F32R)
        cI3 = sb("cI3", [P, P])
        neg_half = sb("neg_half", [P, 20])

        banks = [ctx.enter_context(nc.psum_tensor(f"bank{i}", [P, HALF], F32)) for i in range(8)]

        prologue(nc, ctx, sem, banks, ident, ones, WT_hi, WT_lo, W12_hi, W12_lo, W13_hi, W13_lo,
                 W22, W23, b12, b13, rms_col, bW_row, b22_row, b23_row, v_rows, c_cols,
                 cI2_hi, cI2_lo, cI3, neg_half,
                 x, adj, L0_W1, L0_b1, L0_W2, L0_b2, L0_fusion_w, W, bW, wai, bai, waj, baj,
                 eps2, L2_W1, L2_b1, L2_W2, L2_b2, eps3, L3_W1, L3_b1, rms_w, L3_W2, L3_b2, x_l0)
        layers(nc, sb, sem, banks, ident, ones, WT_hi, WT_lo, W12_hi, W12_lo, W13_hi, W13_lo,
               W22, W23, b12, b13, rms_col, bW_row, b22_row, b23_row, v_rows, c_cols,
               cI2_hi, cI2_lo, cI3, neg_half, x, adj, x_l0, out)


def prologue(nc, ctx, sem, banks, ident, ones, WT_hi, WT_lo, W12_hi, W12_lo, W13_hi, W13_lo,
             W22, W23, b12, b13, rms_col, bW_row, b22_row, b23_row, v_rows, c_cols,
             cI2_hi, cI2_lo, cI3, neg_half,
             x, adj, L0_W1, L0_b1, L0_W2, L0_b2, L0_fusion_w, W, bW, wai, bai, waj, baj,
             eps2, L2_W1, L2_b1, L2_W2, L2_b2, eps3, L3_W1, L3_b1, rms_w, L3_W2, L3_b2, x_l0):
    ROWS = T0 * P
    KH = L0_HID // P
    with ExitStack() as pro:
        def sb(name, shape, dt=F32):
            return pro.enter_context(nc.sbuf_tensor(name, shape, dt))

        W_nat = sb("W_nat", [P, DT, D])
        W12_f, W13_f = sb("W12_f", [P, DT, HID2]), sb("W13_f", [P, DT, HID3])
        wa_cols = sb("wa_cols", [P, 2, DT])
        bW_col = sb("bW_col", [P, DT])
        ba = sb("ba", [P, 2])
        eps_col = sb("eps_col", [P, 2])
        one_eps2 = sb("one_eps2", [P, 1])
        cI2 = sb("cI2", [P, P])
        fus, fus_e = sb("fus", [P, NG]), sb("fus_e", [P, NG])
        fus_m, fus_s, fus_r = sb("fus_m", [P, 1]), sb("fus_s", [P, 1]), sb("fus_r", [P, 1])
        row_mask = sb("row_mask", [1, NG, PER, PAD])
        mw = sb("mw", [P, NG])
        G1 = sb("G1", [P, NG, DT, L0_HID])
        G2 = sb("G2", [P, NG, KH, D])
        g_b1 = sb("g_b1", [P, NG, KH])
        g_b2 = sb("g_b2", [P, NG, D])
        X0 = sb("X0", [P, T0, D])
        A0 = sb("A0", [P, NG, T0 * PER, PAD])
        deg, deg0 = sb("deg", [P, NG * T0]), sb("deg0", [P, NG * T0])
        dinv, dtmp = sb("dinv", [P, NG * T0]), sb("dtmp", [P, NG * T0])
        AT = sb("AT", [P, NG, T0, P])
        XaT = [sb(f"XaT{g}", [P, DT, GRAPHS * group_size(g)]) for g in range(NG)]
        H1 = sb("H1", [P, 2, KH, T0 * PER, PAD])
        Z = sb("Z", [P, 2, T0, D])
        Ot = sb("Ot", [P, 2, D])
        Or = sb("Or", [P, 2, D])

        s_wload = sem("p_weights_loaded")
        s_cload = sem("p_columns_loaded")
        s_gload = sem("p_group_weights_loaded")
        s_zero = sem("p_zeroed")
        s_ident = sem("p_identity")
        s_aload = sem("p_graphs_loaded")
        s_mm = sem("p_bank_written")
        s_ev = sem("p_bank_read")
        s_hmm = sem("p_hidden_written")
        s_hev = sem("p_hidden_read")
        s_dve = sem("p_vector_steps")
        s_mask = sem("p_masks")
        s_deg = sem("p_degrees")
        s_pow = sem("p_powers")
        s_fus = sem("p_fusion_exp")
        s_or = sem("p_group_relu")
        s_acc = sem("p_accumulated")
        s_store = sem("p_stored")

        w_loads, c_loads, a_loads = 5, 15, 2 * GRAPHS
        supports = 4 + NG + DT * NG

        with nc.Block() as block:
            @block.sync
            def _(sp):
                sp.wait_ge(s_zero, 2)
                for b in range(GRAPHS):
                    t, i = b // PER, b % PER
                    rows = slice(PAD * i, PAD * i + L0_NODES)
                    sp.dma_start(A0[rows, 0, b, 0:L0_NODES],
                                 adj[b, 0:L0_NODES, 0:L0_NODES]).then_inc(s_aload, 16)
                    sp.dma_start(X0[rows, t, :], x[b, 0:L0_NODES, :]).then_inc(s_aload, 16)
                sp.dma_start(G1[:], L0_W1.rearrange("g (t p) n -> p g t n", p=P)).then_inc(s_gload, 16)
                sp.dma_start(G2[:], L0_W2.rearrange("g (t p) n -> p g t n", p=P)).then_inc(s_gload, 16)
                sp.dma_start(W12_f[:], L2_W1.rearrange("(t p) n -> p t n", p=P)).then_inc(s_wload, 16)
                sp.dma_start(W13_f[:], L3_W1.rearrange("(t p) n -> p t n", p=P)).then_inc(s_wload, 16)
                sp.dma_start(W22[:], L2_W2.rearrange("(t p) n -> p t n", p=P)).then_inc(s_wload, 16)
                sp.dma_start(W23[:], L3_W2.rearrange("(t p) n -> p t n", p=P)).then_inc(s_wload, 16)
                sp.wait_ge(s_acc, NG * T0)
                for b in range(GRAPHS):
                    t, i = b // PER, b % PER
                    rows = slice(PAD * i, PAD * i + L0_NODES)
                    sp.dma_start(x_l0[b], X0[rows, t, :]).then_inc(s_store, 16)
                sp.wait_ge(s_store, 16 * GRAPHS)
                sp.wait_ge(s_wload, 16 * w_loads)

            @block.scalar
            def _(act):
                act.dma_start(W_nat[:], W.rearrange("(t p) n -> p t n", p=P)).then_inc(s_wload, 16)

                def column(dst, src):
                    act.dma_start(dst, src).then_inc(s_cload, 16)

                with nc.allow_non_contiguous_dma(reason="small columns"):
                    column(wa_cols[:, 0, :], wai.rearrange("a (t p) -> p (a t)", p=P))
                    column(wa_cols[:, 1, :], waj.rearrange("a (t p) -> p (a t)", p=P))
                    column(bW_col[:], bW.rearrange("(t p) -> p t", p=P))
                    column(b12[:], L2_b1.rearrange("(t p) -> p t", p=P))
                    column(b13[:], L3_b1.rearrange("(t p) -> p t", p=P))
                    column(rms_col[:], rms_w.rearrange("(t p) -> p t", p=P))
                    column(g_b1[:], L0_b1.rearrange("g (t p) -> p g t", p=P))
                    column(ba[:, 0:1], row(bai).to_broadcast([P, 1]))
                    column(ba[:, 1:2], row(baj).to_broadcast([P, 1]))
                    column(eps_col[:, 0:1], row(eps2).to_broadcast([P, 1]))
                    column(eps_col[:, 1:2], row(eps3).to_broadcast([P, 1]))
                    column(fus[:], row(L0_fusion_w).to_broadcast([P, NG]))
                    column(bW_row[:], row(bW).to_broadcast([P, D]))
                    column(b22_row[:], row(L2_b2).to_broadcast([P, D]))
                    column(b23_row[:], row(L3_b2).to_broadcast([P, D]))
                    act.dma_start(g_b2[:], L0_b2.rearrange("(a g) n -> a g n", a=1).to_broadcast([P, NG, D]))\
                       .then_inc(s_gload, 16)
                act.wait_ge(s_dve, 2)
                nc.scalar.activation(fus_e[:], fus[:], ACT.Exp, bias=fus_m[:], accum_out=fus_s[:]).then_inc(s_fus, 1)
                def hidden_rows(g):
                    for h in range(KH):
                        n = g * KH + h
                        if g >= 2 and h == 0:
                            act.wait_ge(s_mm, supports + 2 * T0 * (g - 2) + T0)
                        act.wait_ge(s_hmm, n + 1)
                        if n == 0:
                            act.wait_ge(s_zero, 3)
                        at = 0
                        for first, size in GROUP_RUNS[g]:
                            src = banks[6 + n % 2][:, 0:GRAPHS * group_size(g)]\
                                .rearrange("p (b j) -> p b j", b=GRAPHS)[:, :, at:at + size]
                            last = nc.scalar.activation(H1[:, g % 2, h, :, first:first + size], src,
                                                        ACT.Relu, bias=g_b1[:, g, h:h + 1])
                            at += size
                        last.then_inc(s_hev, 1)

                hidden_rows(0)
                hidden_rows(1)
                for g in range(NG):
                    for t in range(T0):
                        i = g * T0 + t
                        act.wait_ge(s_ev, supports + 2 * T0 * g + T0 + t + 1)
                        if i >= 2:
                            act.wait_ge(s_acc, i - 1)
                        nc.scalar.activation(Or[:, i % 2, :], Ot[:, i % 2, :], ACT.Relu,
                                             scale=mw[:, g:g + 1]).then_inc(s_or, 1)
                    if g + 2 < NG:
                        hidden_rows(g + 2)

            @block.gpsimd
            def _(pool):
                nc.gpsimd.memset(A0[:, 0], 0.0).then_inc(s_zero, 1)
                nc.gpsimd.memset(X0[:], 0.0).then_inc(s_zero, 1)
                nc.gpsimd.memset(ident[:], 0.0).then_inc(s_ident, 1)
                nc.gpsimd.memset(ones[:], 1.0).then_inc(s_ident, 1)
                nc.gpsimd.memset(neg_half[:], -0.5).then_inc(s_ident, 1)
                pool.wait_ge(s_ident, 3)
                nc.gpsimd.affine_select(out=ident[:], in_=ident[:], compare_op=ALU.not_equal, fill=1.0, base=0,
                                        pattern=[[-1, P]], channel_multiplier=1).then_inc(s_ident, 1)
                nc.gpsimd.memset(H1[:], 0.0).then_inc(s_zero, 1)
                pool.wait_ge(s_deg, 1)
                nc.gpsimd.tensor_tensor(dtmp[:], dinv[:], neg_half[:], ALU.pow).then_inc(s_pow, 1)
                for i in range(NG * T0):
                    pool.wait_ge(s_or, i + 1)
                    if i >= T0:
                        pool.wait_ge(s_acc, i - T0 + 1)
                    nc.gpsimd.tensor_tensor(X0[:, i % T0, :], X0[:, i % T0, :], Or[:, i % 2, :],
                                            ALU.add).then_inc(s_acc, 1)

            @block.vector
            def _(dve):
                steps = [0]

                def step(ins):
                    steps[0] += 1
                    ins.then_inc(s_dve, 1)
                    dve.wait_ge(s_dve, steps[0])

                dve.wait_ge(s_cload, 16 * c_loads)
                step(nc.vector.reduce_max(fus_m[:], fus[:], axis=AX.X))
                step(nc.vector.tensor_scalar(fus_m[:], fus_m[:], -1.0, None, ALU.mult))
                step(nc.vector.memset(row_mask[:], 0.0))
                for g in range(NG):
                    for first, size in GROUP_RUNS[g]:
                        last = nc.vector.memset(row_mask[:, g, :, first:first + size], 1.0)
                last.then_inc(s_mask, 1)
                step(nc.vector.memset(A0[:, 1:NG], 0.0))
                dve.wait_ge(s_aload, 16 * a_loads)
                dve.wait_ge(s_ident, 4)
                for t in range(T0):
                    blk = A0[:, 0, t * PER:(t + 1) * PER, :]
                    last = nc.vector.tensor_tensor(blk, blk, ident[:].rearrange("p (b j) -> p b j", j=PAD), ALU.add)
                step(last)
                for g in range(1, NG):
                    for first, size in GROUP_RUNS[g]:
                        last = nc.vector.tensor_copy(A0[:, g, :, first:first + size], A0[:, 0, :, first:first + size])
                step(last)
                A_rows = A0[:].rearrange("p g (t b) j -> p (g t) (b j)", b=PER)
                step(nc.vector.tensor_reduce(deg[:], A_rows, AX.X, ALU.add))
                step(nc.vector.tensor_scalar(deg0[:], deg[:], 0.0, None, ALU.is_equal))
                nc.vector.tensor_tensor(dinv[:], deg[:], deg0[:], ALU.add).then_inc(s_deg, 1)
                dve.wait_ge(s_pow, 1)
                step(nc.vector.tensor_scalar(deg0[:], deg0[:], -1.0, 1.0, ALU.mult, ALU.add))
                step(nc.vector.tensor_tensor(dinv[:], dtmp[:], deg0[:], ALU.mult))
                scale = dinv[:].rearrange("p (n a) -> p n a", a=1).to_broadcast([P, NG * T0, P])
                nc.vector.tensor_tensor(A_rows, A_rows, scale, ALU.mult).then_inc(s_deg, 1)

                dve.wait_ge(s_wload, 16 * w_loads)
                for f, hi, lo in ((W12_f, W12_hi, W12_lo), (W13_f, W13_hi, W13_lo)):
                    step(nc.vector.tensor_copy(hi[:], f[:]))
                    nc.vector.tensor_tensor(lo[:], f[:], hi[:].bitcast(F32), ALU.subtract)
                step(nc.vector.tensor_scalar(one_eps2[:], eps_col[:, 0:1], 1.0, None, ALU.add))
                step(nc.vector.tensor_scalar(cI2[:], ident[:], one_eps2[:], None, ALU.mult))
                step(nc.vector.tensor_copy(cI2_hi[:], cI2[:]))
                nc.vector.tensor_tensor(cI2_lo[:], cI2[:], cI2_hi[:].bitcast(F32), ALU.subtract)
                nc.vector.tensor_scalar(cI3[:], ident[:], eps_col[:, 1:2], None, ALU.mult)

                n = [0]

                def bank():
                    dve.wait_ge(s_mm, n[0] + 1)
                    n[0] += 1
                    return banks[(n[0] - 1) % 6]

                src = bank()
                step(nc.vector.tensor_copy(WT_hi[:].rearrange("p t n -> p (t n)"), src[:]))
                nc.vector.tensor_tensor(WT_lo[:].rearrange("p t n -> p (t n)"), src[:],
                                        WT_hi[:].rearrange("p t n -> p (t n)").bitcast(F32),
                                        ALU.subtract).then_inc(s_ev, 1)
                src = bank()
                nc.vector.tensor_copy(v_rows[:].rearrange("p a n -> p (a n)"), src[:]).then_inc(s_ev, 1)
                src = bank()
                nc.vector.tensor_tensor(c_cols[:], src[:, 0:2], ba[:], ALU.add).then_inc(s_ev, 1)
                dve.wait_ge(s_fus, 1)
                step(nc.vector.reciprocal(fus_r[:], fus_s[:]))
                step(nc.vector.tensor_scalar(fus_e[:], fus_e[:], fus_r[:], None, ALU.mult))
                src = bank()
                nc.vector.tensor_tensor(mw[:], src[:, 0:NG], fus_e[:], ALU.mult).then_inc(s_ev, 1)
                for g in range(NG):
                    src = bank()
                    other = dinv[:, g * T0:(g + 1) * T0].rearrange("p (t a) -> p t a", a=1).to_broadcast([P, T0, P])
                    nc.vector.tensor_tensor(AT[:, g], src[:].rearrange("p (t n) -> p t n", n=P), other,
                                            ALU.mult).then_inc(s_ev, 1)
                for g in range(NG):
                    for d in range(DT):
                        src = bank()
                        nc.vector.tensor_copy(XaT[g][:, d, :], src[:, 0:GRAPHS * group_size(g)]).then_inc(s_ev, 1)
                dve.wait_ge(s_gload, 48)
                i = 0
                for g in range(NG):
                    for t in range(T0):
                        src = bank()
                        nc.vector.tensor_copy(Z[:, g % 2, t, :], src[:, 0:D]).then_inc(s_ev, 1)
                    for t in range(T0):
                        src = bank()
                        if i >= 2:
                            dve.wait_ge(s_or, i - 1)
                        nc.vector.tensor_tensor(Ot[:, i % 2, :], src[:, 0:D], g_b2[:, g, :], ALU.add)\
                            .then_inc(s_ev, 1)
                        i += 1

            @block.tensor
            def _(pe):
                n = [0]

                def bank():
                    if n[0] >= 6:
                        pe.wait_ge(s_ev, n[0] - 5)
                    n[0] += 1
                    return banks[(n[0] - 1) % 6]

                pe.wait_ge(s_ident, 4)
                pe.wait_ge(s_wload, 16 * w_loads)
                pe.wait_ge(s_cload, 16 * c_loads)
                dst = bank()
                for i in range(DT):
                    for o in range(DT):
                        last = nc.tensor.transpose(dst[:, i * D + o * P:i * D + (o + 1) * P],
                                                   W_nat[:, o, i * P:(i + 1) * P], ident[:])
                last.then_inc(s_mm, 1)
                dst = bank()
                for a in range(2):
                    for o in range(DT):
                        last = nc.tensor.matmul(dst[:, a * D:(a + 1) * D], wa_cols[:, a, o:o + 1].to_broadcast([P, P]),
                                                W_nat[:, o, :], start=(o == 0), stop=(o == DT - 1))
                last.then_inc(s_mm, 1)
                dst = bank()
                for a in range(2):
                    for o in range(DT):
                        last = nc.tensor.matmul(dst[:, a:a + 1], wa_cols[:, a, o:o + 1].to_broadcast([P, P]),
                                                bW_col[:, o:o + 1], start=(o == 0), stop=(o == DT - 1))
                last.then_inc(s_mm, 1)
                pe.wait_ge(s_mask, 1)
                dst = bank()
                for g in range(NG):
                    last = nc.tensor.matmul(dst[:, g:g + 1], row_mask[:, g].rearrange("p b j -> p (b j)"),
                                            ones[0:1, 0:1], start=True, stop=True)
                last.then_inc(s_mm, 1)
                pe.wait_ge(s_deg, 2)
                for g in range(NG):
                    dst = bank()
                    for t in range(T0):
                        last = nc.tensor.transpose(dst[:, t * P:(t + 1) * P],
                                                   A0[:, g, t * PER:(t + 1) * PER, :].rearrange("p b j -> p (b j)"),
                                                   ident[:])
                    last.then_inc(s_mm, 1)
                for g in range(NG):
                    size = group_size(g)
                    for d in range(DT):
                        dst = bank()
                        if d == 0:
                            pe.wait_ge(s_ev, 4 + g + 1)
                        for t in range(T0):
                            at = 0
                            for first, run in GROUP_RUNS[g]:
                                cols = dst[:, 0:GRAPHS * size].rearrange("p (b j) -> p b j", b=GRAPHS)
                                last = nc.tensor.matmul(
                                    cols[:, t * PER:(t + 1) * PER, at:at + run], X0[:, t, d * P:(d + 1) * P],
                                    AT[:, g, t, :].rearrange("p (b j) -> p b j", j=PAD)[:, :, first:first + run],
                                    start=True, stop=True)
                                at += run
                        last.then_inc(s_mm, 1)
                pe.wait_ge(s_gload, 48)
                h = 0

                def hidden(g, h):
                    size = GRAPHS * group_size(g)
                    pe.wait_ge(s_ev, 4 + NG + DT * (g + 1))
                    for m in range(KH):
                        if h >= 2:
                            pe.wait_ge(s_hev, h - 1)
                        for d in range(DT):
                            last = nc.tensor.matmul(banks[6 + h % 2][:, 0:size], G1[:, g, d, m * P:(m + 1) * P],
                                                    XaT[g][:, d, :], start=(d == 0), stop=(d == DT - 1))
                        last.then_inc(s_hmm, 1)
                        h += 1
                    return h

                h = hidden(0, h)
                for g in range(NG):
                    if g + 1 < NG:
                        h = hidden(g + 1, h)
                    pe.wait_ge(s_hev, KH * (g + 1))
                    for t in range(T0):
                        dst = bank()
                        for m in range(KH):
                            rows = H1[:, g % 2, m, t * PER:(t + 1) * PER, :].rearrange("p b j -> p (b j)")
                            last = nc.tensor.matmul(dst[:, 0:D], rows, G2[:, g, m, :], start=(m == 0), stop=(m == KH - 1))
                        last.then_inc(s_mm, 1)
                    pe.wait_ge(s_ev, n[0])
                    for t in range(T0):
                        dst = bank()
                        nc.tensor.matmul(dst[:, 0:D], AT[:, g, t, :], Z[:, g % 2, t, :],
                                         start=True, stop=True).then_inc(s_mm, 1)


def layers(nc, sb, sem, banks, ident, ones, WT_hi, WT_lo, W12_hi, W12_lo, W13_hi, W13_lo,
           W22, W23, b12, b13, rms_col, bW_row, b22_row, b23_row, v_rows, c_cols,
           cI2_hi, cI2_lo, cI3, neg_half, x, adj, x_l0, out):
    att = sb("att", [P, NT, NODES])
    adj_col = sb("adj_col", [P, CR, NT, P])
    mt_hi, mt_lo = sb("mt_hi", [P, NT, NODES], F32R), sb("mt_lo", [P, NT, NODES], F32R)
    x_res = sb("x_res", [P, NT, D])
    x_hi, x_lo = sb("x_hi", [P, NT, D], F32R), sb("x_lo", [P, NT, D], F32R)
    a_hi, a_lo = sb("a_hi", [P, DT, HALF], F32R), sb("a_lo", [P, DT, HALF], F32R)
    hid = sb("hid", [P, 2, HT3, QUARTER])
    sq = sb("sq", [P, 2, QUARTER])
    bias_tmp = sq[:, 0, :]
    sq_sum = sb("sq_sum", [P, 2, QUARTER])
    aj_row, aj_row2 = sb("aj_row", [P, NODES]), sb("aj_row2", [P, NODES])
    neg_mask = sb("neg_mask", [P, NODES])
    prod = neg_mask[:, 0:D]
    x_raw = sb("x_raw", [P, 2, D])
    stat = sb("stat", [P, 2, 6])
    mv = sb("mv", [P, NT, 2])
    ve, rstd = sb("ve", [P, NT]), sb("rstd", [P, NT])
    stat0 = sb("stat0", [P, 2, 6])
    mv0, ve0, rstd0 = sb("mv0", [P, NT, 2]), sb("ve0", [P, NT]), sb("rstd0", [P, NT])
    qi, qj = sb("qi", [P, NT]), sb("qj", [P, NT])
    ai, aj = sb("ai", [P, NT]), sb("aj", [P, NT])
    shift, floor = sb("shift", [P, NT]), sb("floor", [P, NT])
    top, neg_top = sb("top", [P, NT]), sb("neg_top", [P, NT])
    total, sink, sink_arg = sb("total", [P, NT]), sb("sink", [P, NT]), sb("sink_arg", [P, NT])
    den, rden, covered = sb("den", [P, NT]), sb("rden", [P, NT]), sb("covered", [P, NT])
    held, held_pool = sb("held", [P, 8]), sb("held_pool", [P, 2 * NT])
    ms, rms = sb("ms", [P, 2, 2]), sb("rms", [P, 2, 2])

    agg_bank = [[banks[0], banks[2]], [banks[1], banks[3]]]
    hid_bank = [banks[0], banks[1]]
    turn_bank = [banks[4], banks[5]]
    out_bank = [banks[6], banks[7]]

    s_att_in = [sem(f"adj_rows_loaded{t}") for t in range(NT)]
    s_col_in = [sem(f"adj_cols_loaded{i}") for i in range(CR)]
    s_x_in = [sem(f"x_loaded{t}") for t in range(NT)]
    s_raw_in = [sem(f"x_raw_loaded{i}") for i in range(2)]
    s_stored = [sem(f"out_stored{t}") for t in range(NT)]
    s_turned = [sem(f"turn_bank_written{i}") for i in range(2)]
    s_turn_hi = [sem(f"turn_bank_hi_taken{i}") for i in range(2)]
    s_turn_free = [sem(f"turn_bank_lo_taken{i}") for i in range(2)]
    s_agg = [None] + [sem(f"agg_steps_l{n}") for n in (1, 2, 3)]
    s_agg_h0 = sem("agg_first_half")
    s_a_hi, s_a_lo = sem("a_hi_ready"), sem("a_lo_ready")
    s_hid_mm = sem("hidden_bank_written")
    s_hid_act, s_hid3 = sem("relu_or_square"), sem("hidden3_bank_read")
    s_sq_sum, s_rms = sem("squares_added"), sem("rms_factor")
    s_scaled, s_silu = sem("hidden_scaled"), sem("hidden_silu")
    s_out_mm, s_out_read = sem("out_bank_written"), sem("out_bank_read")
    s_var, s_rstd, s_y = sem("variance"), sem("rstd"), sem("normed")
    s_y0 = sem("normed0")
    s_x_hi, s_x_lo, s_bias = sem("x_hi"), sem("x_lo"), sem("bias_added")
    s_diag = sem("diagonal_added")
    s_raw_used, s_var0, s_rstd0 = sem("x_raw_used"), sem("variance0"), sem("rstd0")
    s_aj, s_masked = sem("aj_columns"), sem("scores_masked")
    s_top, s_exp, s_sink_arg, s_sink, s_den = sem("row_tops"), sem("exps"), sem("sink_arg"), sem("sink"), sem("denominators")
    s_dve = sem("vector_steps")

    LN = NT
    TURNS = 2 * NT + 1 + NQ
    TURN_AJ, TURN_RMS = 2 * NT, 2 * NT + 1
    AGG = NT - 1
    HID = NQ * (HT2 + HT3)
    STEPS_FIRST = 3 * NT + 5 + 2 * NT + 2
    STEPS = STEPS_FIRST + 3 * 2 * NT

    def sum_at(q):
        return 2 if q == 1 else 0

    def row_at(q):
        return sum_at(q) + 3

    def steps_by(k):
        return min(k + 1, AGG)

    def adj_use(k):
        return NT + k

    def turn(b, last, u):
        return 1 + b * TURNS + u - (1 if last and u > TURN_AJ else 0)

    def split_count(b, last, u):
        return 1 + b * TURN_RMS + u - (1 if last and u > TURN_AJ else 0)

    with nc.Block() as block:
        @block.sync
        def _(sp):
            def load_x(dst, b, t, done):
                if t == 0:
                    sp.dma_start(dst[0:L0_NODES], x_l0[b]).then_inc(done, 16)
                    sp.dma_start(dst[L0_NODES:P], x[b, L0_NODES:P, :]).then_inc(done, 16)
                else:
                    sp.dma_start(dst, x[b, t * P:(t + 1) * P, :]).then_inc(done, 16)

            def load_raw(b, t, prior=True):
                if t >= 2:
                    sp.wait_ge(s_raw_used, b * NT + t - 1)
                elif prior:
                    sp.wait_ge(s_raw_used, b * NT)
                load_x(x_raw[:, t % 2, :], b, t, s_raw_in[t % 2])

            def load_row(b, t):
                sp.dma_start(att[:, t, :], adj[b, t * P:(t + 1) * P, :]).then_inc(s_att_in[t], 16)

            def load_col(b, k):
                sp.dma_start(adj_col[:, k % CR], adj[b, :, k * P:(k + 1) * P].rearrange("(t p) m -> p t m", p=P))\
                  .then_inc(s_col_in[k % CR], 16)

            def graph(b, last):
                load_col(b, 0)
                load_col(b, 1)
                load_col(b, 2)
                if not last:
                    for t in range(4):
                        load_raw(b + 1, t)
                    sp.wait_ge(s_turned[1], turn(b, last, NT))
                    load_row(b + 1, 0)
                    load_row(b + 1, 1)
                for k in range(CR, NT):
                    sp.wait_ge(s_turned[1], turn(b, last, adj_use(k - CR) + 1))
                    load_col(b, k)
                    if not last:
                        if k == 3:
                            load_raw(b + 1, 4)
                        if 3 <= k < 6:
                            load_raw(b + 1, k + 2)
                        load_row(b + 1, k - 1)
                if not last:
                    load_row(b + 1, NT - 1)
                for t in range(NT):
                    sp.wait_ge(s_y, b * 3 * LN + 2 * LN + t + 1)
                    sp.dma_start(out[b, t * P:(t + 1) * P, :], x_res[:, t, :]).then_inc(s_stored[t], 16)
                    if not last:
                        for done in {2: (0,), 3: (1, 2, 3), NT - 2: (4,), NT - 1: (5, 6, 7)}.get(t, ()):
                            next_x(b, done)

            def next_x(b, t):
                sp.wait_ge(s_stored[t], (b + 1) * 16)
                load_x(x_res[:, t, :], b + 1, t, s_x_in[t])

            for t in range(NT):
                load_raw(0, t, prior=False)
            for t in range(NT):
                load_row(0, t)
            for t in range(NT):
                load_x(x_res[:, t, :], 0, t, s_x_in[t])
            with sp.Fori(0, GRAPHS - 1) as b:
                graph(b, False)
            graph(GRAPHS - 1, True)
            for t in range(NT):
                sp.wait_ge(s_stored[t], GRAPHS * 16)

        @block.tensor
        def _(pe):
            def turn_begin(i, b, last, u):
                if i == 0:
                    pe.wait_ge(s_turn_free[0], turn(b, last, u))
                else:
                    pe.wait_ge(s_turn_free[1], split_count(b, last, min(u, TURN_RMS)))
                    if u > TURN_RMS:
                        pe.wait_ge(s_scaled, b * NQ * HT3 + (u - TURN_RMS) * HT3)

            def turn_att(b, last, k):
                for i in range(2):
                    turn_begin(i, b, last, k)
                    for j in range(4):
                        mm = nc.tensor.transpose(turn_bank[i][:, j * P:(j + 1) * P],
                                                 att[:, 4 * i + j, k * P:(k + 1) * P], ident[:])
                    mm.then_inc(s_turned[i], 1)

            def turn_col(b, last, k):
                pe.wait_ge(s_diag, b * NT + k + 1)
                for i in range(2):
                    turn_begin(i, b, last, adj_use(k))
                    for j in range(4):
                        mm = nc.tensor.transpose(turn_bank[i][:, j * P:(j + 1) * P],
                                                 adj_col[:, k % CR, 4 * i + j, :], ident[:])
                    mm.then_inc(s_turned[i], 1)

            def aj_rows(aj_count, begin):
                pe.wait_ge(s_aj, aj_count)
                for i in range(2):
                    begin(i)
                    for j in range(4):
                        t = 4 * i + j
                        mm = nc.tensor.matmul(turn_bank[i][:, j * P:(j + 1) * P], aj[:, t:t + 1].to_broadcast([P, P]),
                                              ident[:], start=True, stop=True)
                    mm.then_inc(s_turned[i], 1)

            def agg_step(layer, k, h, first, last_k):
                for d in range(DT):
                    dst = agg_bank[d][h]
                    cols = slice(h * HALF, (h + 1) * HALF)
                    hi, lo = x_hi[:, k, d * P:(d + 1) * P], x_lo[:, k, d * P:(d + 1) * P]
                    extra = layer == 2 and k // 4 == h
                    nc.tensor.matmul(dst[:], hi, mt_hi[:, k, cols], start=first, stop=False)
                    nc.tensor.matmul(dst[:], hi, mt_lo[:, k, cols], start=False, stop=False)
                    mm = nc.tensor.matmul(dst[:], lo, mt_hi[:, k, cols], start=False, stop=last_k and not extra,
                                          skip_group_check=False)
                    if extra:
                        own = dst[:, (k % 4) * P:(k % 4 + 1) * P]
                        nc.tensor.matmul(own, hi, cI2_hi[:], start=False, stop=False)
                        nc.tensor.matmul(own, hi, cI2_lo[:], start=False, stop=False)
                        mm = nc.tensor.matmul(own, lo, cI2_hi[:], start=False, stop=last_k)
                return mm

            def aggregate(b, last, layer):
                turned = {1: turn_att, 2: turn_col}.get(layer)
                for k in range(NT):
                    if turned and k + 2 < NT:
                        turned(b, last, k + 2)
                    if turned:
                        use = k if layer == 1 else adj_use(k)
                        pe.wait_ge(s_turn_free[0], turn(b, last, use + 1))
                        pe.wait_ge(s_turn_free[1], split_count(b, last, use + 1))
                    pe.wait_ge(s_x_lo, b * 3 * LN + (layer - 1) * LN + k + 1)
                    if k < NT - 2:
                        agg_step(layer, k, 0, k == 0, False)
                        agg_step(layer, k, 1, k == 0, False).then_inc(s_agg[layer], 1)
                agg_step(layer, NT - 2, 0, False, False)
                agg_step(layer, NT - 1, 0, False, True).then_inc(s_agg_h0, 1)
                agg_step(layer, NT - 2, 1, False, False)
                agg_step(layer, NT - 1, 1, False, True).then_inc(s_agg[layer], 1)

            def split_product(dst, a_cols, w_hi, w_lo, w_cols, hidden):
                for d in range(DT):
                    ah, al = a_hi[:, d, a_cols], a_lo[:, d, a_cols]
                    wh, wl = w_hi[:, d, w_cols], w_lo[:, d, w_cols]
                    for n, (l, r) in enumerate(((wh, ah), (wh, al), (wl, ah)) if hidden else ((ah, wh), (ah, wl), (al, wh))):
                        mm = nc.tensor.matmul(dst, l, r, start=(d == 0 and n == 0), stop=(d == DT - 1 and n == 2))
                return mm

            def a_ready(b, layer, h):
                pe.wait_ge(s_a_lo, b * 6 * DT + ((layer - 1) * 2 + h + 1) * DT)

            def out_free(b, i):
                if i >= 2:
                    pe.wait_ge(s_out_read, b * 3 * LN + i - 1)

            def attention_out(b, t):
                out_free(b, t)
                mm = split_product(out_bank[t % 2][:, 0:D], slice((t % 4) * P, (t % 4 + 1) * P),
                                   WT_hi, WT_lo, slice(0, D), False)
                mm.then_inc(s_out_mm, 1)

            def hidden_tile(b, layer, q, m):
                i = (0 if layer == 2 else NQ * HT2) + q * (HT2 if layer == 2 else HT3) + m
                if i >= NQ * HT2 + 2:
                    pe.wait_ge(s_hid3, b * NQ * HT3 + i - NQ * HT2 - 1)
                elif i >= 2:
                    pe.wait_ge(s_hid_act, b * HID + i - 1)
                w_hi, w_lo = (W12_hi, W12_lo) if layer == 2 else (W13_hi, W13_lo)
                mm = split_product(hid_bank[i % 2][:, 0:QUARTER], slice((q % 2) * QUARTER, (q % 2 + 1) * QUARTER),
                                   w_hi, w_lo, slice(m * P, (m + 1) * P), True)
                mm.then_inc(s_hid_mm, 1)

            def second_product(b, layer, q, between=None):
                W2, tiles = (W22, HT2) if layer == 2 else (W23, HT3)
                for j in range(2):
                    out_free(b, (layer - 1) * NT + 2 * q + j)
                for m in range(tiles):
                    if layer == 2:
                        pe.wait_ge(s_hid_act, b * HID + q * HT2 + m + 1)
                    else:
                        pe.wait_ge(s_silu, b * NQ * HT3 + q * HT3 + m + 1)
                    for j in range(2):
                        mm = nc.tensor.matmul(out_bank[j][:, 0:D], hid[:, q % 2, m, j * P:(j + 1) * P], W2[:, m, :],
                                              start=(m == 0), stop=(m == tiles - 1))
                        if m == tiles - 1:
                            mm.then_inc(s_out_mm, 1)
                    if between and m in between:
                        between[m]()

            def rms_sum(b, last, q):
                pe.wait_ge(s_sq_sum, b * NQ * (HT3 - 1) + (q + 1) * (HT3 - 1))
                turn_begin(0, b, last, TURN_RMS + q)
                for j in range(2):
                    mm = nc.tensor.matmul(turn_bank[0][:, j:j + 1], sq_sum[:, q % 2, j * P:(j + 1) * P], ones[:, 0:1],
                                          start=True, stop=True)
                mm.then_inc(s_turned[0], 1)

            def rms_row(b, last, q):
                pe.wait_ge(s_rms, b * NQ + q + 1)
                turn_begin(1, b, last, TURN_RMS + q)
                for j in range(2):
                    mm = nc.tensor.matmul(turn_bank[1][:, j * P:(j + 1) * P],
                                          rms[:, q % 2, j:j + 1].to_broadcast([P, P]), ident[:], start=True, stop=True)
                mm.then_inc(s_turned[1], 1)

            def graph(b, last):
                aggregate(b, last, 1)
                turn_col(b, last, 0)
                a_ready(b, 1, 0)
                for t in range(NT // 2):
                    attention_out(b, t)
                turn_col(b, last, 1)
                a_ready(b, 1, 1)
                for t in range(NT // 2, NT):
                    attention_out(b, t)
                aggregate(b, last, 2)
                if not last:
                    aj_rows(b + 2, lambda i: turn_begin(i, b, last, TURN_AJ))
                a_ready(b, 2, 0)
                for q in range(NQ):
                    if q == 2:
                        a_ready(b, 2, 1)
                    for m in range(HT2):
                        hidden_tile(b, 2, q, m)
                    if q >= 1:
                        second_product(b, 2, q - 1)
                second_product(b, 2, NQ - 1)
                aggregate(b, last, 3)
                a_ready(b, 3, 0)
                for q in range(NQ):
                    if q == 2:
                        a_ready(b, 3, 1)
                    for m in range(HT3):
                        hidden_tile(b, 3, q, m)
                        if q >= 1 and m == sum_at(q):
                            rms_sum(b, last, q - 1)
                        if q >= 1 and m == row_at(q):
                            rms_row(b, last, q - 1)
                    if q == NQ - 1:
                        second_product(b, 3, q - 1, {2: lambda: rms_sum(b, last, NQ - 1),
                                                     6: lambda: rms_row(b, last, NQ - 1)})
                    elif q >= 1:
                        second_product(b, 3, q - 1)
                if last:
                    second_product(b, 3, NQ - 1)
                else:
                    second_product(b, 3, NQ - 1, {4: lambda: first_turn(b + 1)})
                    turn_att(b + 1, False, 1)

            def first_turn(b):
                pe.wait_ge(s_exp, (b + 1) * NT)
                pe.wait_ge(s_scaled, b * NQ * HT3)
                turn_att(b, False, 0)

            pe.sem_inc(s_agg[3], AGG)
            aj_rows(1, lambda i: None)
            pe.wait_ge(s_exp, NT)
            turn_att(0, False, 0)
            turn_att(0, False, 1)
            with pe.Fori(0, GRAPHS - 1) as b:
                graph(b, False)
            graph(GRAPHS - 1, True)

        @block.scalar
        def _(act):
            def turn_hi(b, last, use, k):
                for i in range(2):
                    act.wait_ge(s_turned[i], turn(b, last, use + 1))
                    nc.scalar.activation(mt_hi[:, k, i * HALF:(i + 1) * HALF], turn_bank[i][:], ACT.Copy)\
                      .then_inc(s_turn_hi[i], 1)

            def take_att(b, last, k):
                act.wait_ge(s_agg[3], b * AGG + steps_by(k))
                turn_hi(b, last, k, k)

            def take_col(b, last, k):
                act.wait_ge(s_agg[1], b * AGG + steps_by(k))
                turn_hi(b, last, adj_use(k), k)

            def aj_copy(count):
                for i in range(2):
                    act.wait_ge(s_turned[i], count + 1)
                    nc.scalar.activation(aj_row[:, i * HALF:(i + 1) * HALF], turn_bank[i][:], ACT.Copy)\
                      .then_inc(s_turn_hi[i], 1)

            def agg_hi(b, layer, h):
                if h == 0:
                    act.wait_ge(s_agg_h0, b * 3 + layer)
                else:
                    act.wait_ge(s_agg[layer], (b + (1 if layer == 3 else 0)) * AGG + AGG)
                if h == 1:
                    used, count = {1: (s_out_mm, b * 3 * NT + NT // 2),
                                   2: (s_hid_mm, b * HID + NQ // 2 * HT2),
                                   3: (s_hid_mm, b * HID + NQ * HT2 + NQ // 2 * HT3)}[layer]
                    act.wait_ge(used, count)
                for d in range(DT):
                    nc.scalar.activation(a_hi[:, d, :], agg_bank[d][h][:], ACT.Copy).then_inc(s_a_hi, 1)

            def x_high(b, norm, t):
                if norm == 0:
                    act.wait_ge(s_y0, b * LN + t + 1)
                else:
                    act.wait_ge(s_y, b * 3 * LN + (norm - 1) * LN + t + 1)
                nc.scalar.activation(x_hi[:, t, :], x_res[:, t, :], ACT.Copy).then_inc(s_x_hi, 1)

            def exp(b, t):
                act.wait_ge(s_top, b * NT + t + 1)
                nc.scalar.activation(att[:, t, :], att[:, t, :], ACT.Exp, bias=neg_top[:, t:t + 1],
                                     accum_out=total[:, t:t + 1]).then_inc(s_exp, 1)

            def sink_exp(b):
                act.wait_ge(s_sink_arg, b + 1)
                nc.scalar.activation(sink[:], sink_arg[:], ACT.Exp).then_inc(s_sink, 1)

            def relu(b, q):
                for m in range(HT2):
                    i = q * HT2 + m
                    act.wait_ge(s_hid_mm, b * HID + i + 1)
                    nc.scalar.activation(hid[:, q % 2, m, :], hid_bank[i % 2][:, 0:QUARTER], ACT.Relu,
                                         bias=b12[:, m:m + 1]).then_inc(s_hid_act, 1)

            def square(b, q, m):
                act.wait_ge(s_hid3, b * NQ * HT3 + q * HT3 + m + 1)
                n = q * (HT3 - 1) + m
                if m == 0:
                    dst = sq_sum[:, q % 2, :]
                else:
                    if m >= 3:
                        act.wait_ge(s_sq_sum, b * NQ * (HT3 - 1) + n - 2)
                    elif q >= 1:
                        act.wait_ge(s_sq_sum, b * NQ * (HT3 - 1) + q * (HT3 - 1))
                    dst = sq[:, m % 2, :]
                nc.scalar.activation(dst, hid[:, q % 2, m, :], ACT.Square).then_inc(s_hid_act, 1)

            def silu(b, q, m):
                act.wait_ge(s_scaled, b * NQ * HT3 + q * HT3 + m + 1)
                nc.scalar.activation(hid[:, q % 2, m, :], hid[:, q % 2, m, :], ACT.Silu).then_inc(s_silu, 1)

            def graph(b, last):
                for k in range(NT):
                    if k >= 1:
                        take_att(b, last, k)
                    if k + 2 < NT:
                        x_high(b, 0, k + 2)
                agg_hi(b, 1, 0)
                take_col(b, last, 0)
                agg_hi(b, 1, 1)
                take_col(b, last, 1)
                take_col(b, last, 2)
                x_high(b, 1, 0)
                x_high(b, 1, 1)
                for k in range(3, NT):
                    take_col(b, last, k)
                    x_high(b, 1, k - 1)
                x_high(b, 1, NT - 1)
                agg_hi(b, 2, 0)
                if not last:
                    aj_copy(turn(b, last, TURN_AJ))
                relu(b, 0)
                relu(b, 1)
                agg_hi(b, 2, 1)
                if not last:
                    exp(b + 1, 0)
                relu(b, 2)
                x_high(b, 2, 0)
                x_high(b, 2, 1)
                if not last:
                    exp(b + 1, 1)
                relu(b, 3)
                x_high(b, 2, 2)
                x_high(b, 2, 3)
                if not last:
                    exp(b + 1, 2)
                x_high(b, 2, 4)
                x_high(b, 2, 5)
                if not last:
                    exp(b + 1, 3)
                x_high(b, 2, 6)
                x_high(b, 2, 7)
                if not last:
                    for t in range(4, NT):
                        exp(b + 1, t)
                agg_hi(b, 3, 0)
                if not last:
                    sink_exp(b + 1)
                for q in range(NQ):
                    for m in range(HT3):
                        square(b, q, m)
                        if q >= 1 and m >= row_at(q) + 2:
                            silu(b, q - 1, m - row_at(q) - 2)
                    if q == 1:
                        agg_hi(b, 3, 1)
                    if q >= 1:
                        for m in range(HT3 - row_at(q) - 2, HT3):
                            silu(b, q - 1, m)
                for m in range(HT3):
                    silu(b, NQ - 1, m)
                if not last:
                    first_tiles(b + 1)

            def first_tiles(b):
                x_high(b, 0, 0)
                take_att(b, False, 0)
                x_high(b, 0, 1)

            aj_copy(0)
            for t in range(NT):
                exp(0, t)
            sink_exp(0)
            first_tiles(0)
            with act.Fori(0, GRAPHS - 1) as b:
                graph(b, False)
            graph(GRAPHS - 1, True)

        @block.gpsimd
        def _(pool):
            def hold(place):
                nc.gpsimd.tensor_tensor(held_pool[:, place:place + 1], ones[:, 0:1], ones[:, 1:2], ALU.add)

            def rstd_of(b, norm, t):
                pool.wait_ge(s_var, b * 3 * LN + (norm - 1) * LN + t + 1)
                nc.gpsimd.tensor_tensor(rstd[:, t:t + 1], ve[:, t:t + 1], neg_half[:, 0:1], ALU.pow).then_inc(s_rstd, 1)

            def x_low(b, norm, t):
                pool.wait_ge(s_x_hi, b * 3 * LN + norm * LN + t + 1)
                nc.gpsimd.tensor_tensor(x_lo[:, t, :], x_res[:, t, :], x_hi[:, t, :].bitcast(F32),
                                        ALU.subtract).then_inc(s_x_lo, 1)

            def add_bias(b, norm, t):
                if norm == 0:
                    if t == 0:
                        pool.wait_ge(s_den, b + 1)
                    if t >= 1:
                        pool.wait_ge(s_bias, b * 4 * LN + 2 * t)
                    hold(NT + t)
                    nc.gpsimd.tensor_scalar(bias_tmp, bW_row[:], covered[:, t:t + 1], None, ALU.mult)\
                      .then_inc(s_bias, 1)
                    bias = bias_tmp
                    pool.wait_ge(s_bias, b * 4 * LN + 2 * t + 1)
                else:
                    bias = (b22_row if norm == 1 else b23_row)[:]
                nc.gpsimd.tensor_tensor(x_res[:, t, :], x_res[:, t, :], bias, ALU.add).then_inc(s_bias, 1)

            def diagonal(b, k):
                pool.wait_ge(s_col_in[k % CR], b * 16 * len(range(k % CR, NT, CR)) + 16 * (k // CR + 1))
                own = adj_col[:, k % CR, k, :]
                nc.gpsimd.tensor_tensor(own, own, cI3[:], ALU.add).then_inc(s_diag, 1)

            def rstd0_of(b):
                pool.wait_ge(s_var0, b + 1)
                nc.gpsimd.tensor_tensor(rstd0[:], ve0[:], neg_half[:, 0:NT], ALU.pow).then_inc(s_rstd0, 1)

            def add_square(b, q, m):
                pool.wait_ge(s_hid_act, b * HID + NQ * HT2 + q * HT3 + m + 1)
                if m >= 2:
                    pool.wait_ge(s_sq_sum, b * NQ * (HT3 - 1) + q * (HT3 - 1) + m - 1)
                total_sq = sq_sum[:, q % 2, :]
                nc.gpsimd.tensor_tensor(total_sq, total_sq, sq[:, m % 2, :], ALU.add).then_inc(s_sq_sum, 1)

            def rms_of(b, last, q):
                pool.wait_ge(s_turn_free[0], turn(b, last, TURN_RMS + q + 1))
                nc.gpsimd.tensor_tensor(rms[:, q % 2, :], ms[:, q % 2, :], neg_half[:, 0:2], ALU.pow).then_inc(s_rms, 1)

            def graph(b, last):
                for t in range(2, NT):
                    x_low(b, 0, t)
                    add_bias(b, 0, t)
                diagonal(b, 0)
                diagonal(b, 1)
                diagonal(b, 2)
                for t in range(3):
                    rstd_of(b, 1, t)
                for t in range(NT):
                    x_low(b, 1, t)
                    add_bias(b, 1, t)
                    if t + 3 < NT:
                        diagonal(b, t + 3)
                        rstd_of(b, 1, t + 3)
                if not last:
                    rstd0_of(b + 1)
                for q in range(NQ):
                    rstd_of(b, 2, 2 * q)
                    rstd_of(b, 2, 2 * q + 1)
                    for t in (2 * q, 2 * q + 1):
                        x_low(b, 2, t)
                        add_bias(b, 2, t)
                for q in range(NQ):
                    for m in range(1, HT3):
                        add_square(b, q, m)
                        if q >= 1 and m == sum_at(q) + 1:
                            rms_of(b, last, q - 1)
                    if q >= 2:
                        rstd_of(b, 3, 2 * q - 4)
                        rstd_of(b, 3, 2 * q - 3)
                rms_of(b, last, NQ - 1)
                rstd_of(b, 3, NT - 4)
                rstd_of(b, 3, NT - 3)
                if not last:
                    first_tiles(b + 1)
                rstd_of(b, 3, NT - 2)
                rstd_of(b, 3, NT - 1)

            def first_tiles(b):
                for t in range(2):
                    x_low(b, 0, t)
                    add_bias(b, 0, t)

            rstd0_of(0)
            first_tiles(0)
            with pool.Fori(0, GRAPHS - 1) as b:
                graph(b, False)
            graph(GRAPHS - 1, True)

        @block.vector
        def _(dve):
            taken = [0]

            def step(base, ins):
                taken[0] += 1
                ins.then_inc(s_dve, 1)
                dve.wait_ge(s_dve, base + taken[0])

            holds = [0]

            def hold():
                holds[0] = (holds[0] + 1) % 8
                nc.vector.tensor_copy(held[:, holds[0]:holds[0] + 1], ones[:, 0:1])

            def turn_lo(b, last, use, k):
                for i in range(2):
                    dve.wait_ge(s_turn_hi[i], split_count(b, last, use + 1))
                    cols = slice(i * HALF, (i + 1) * HALF)
                    nc.vector.tensor_tensor(mt_lo[:, k, cols], turn_bank[i][:], mt_hi[:, k, cols].bitcast(F32),
                                            ALU.subtract).then_inc(s_turn_free[i], 1)

            def aj_scaled(count):
                for i in range(2):
                    dve.wait_ge(s_turn_hi[i], count + 1)
                    nc.vector.tensor_scalar(aj_row2[:, i * HALF:(i + 1) * HALF], turn_bank[i][:], SLOPE, None,
                                            ALU.mult).then_inc(s_turn_free[i], 1)

            def agg_lo(b, layer, h):
                n = ((layer - 1) * 2 + h) * DT
                for d in range(DT):
                    dve.wait_ge(s_a_hi, b * 6 * DT + n + d + 1)
                    nc.vector.tensor_tensor(a_lo[:, d, :], agg_bank[d][h][:], a_hi[:, d, :].bitcast(F32),
                                            ALU.subtract).then_inc(s_a_lo, 1)

            def residual(b, layer, t):
                i = (layer - 1) * NT + t
                dve.wait_ge(s_out_mm, b * 3 * LN + i + 1)
                dve.wait_ge(s_bias, b * 4 * LN + (2 * t + 2 if layer == 1 else layer * LN + t + 1))
                src = out_bank[i % 2][:, 0:D]
                if layer == 1:
                    ins = nc.vector.scalar_tensor_tensor(out=x_res[:, t, :], in0=src, scalar=rden[:, t:t + 1],
                                                         in1=x_res[:, t, :], op0=ALU.mult, op1=ALU.add)
                else:
                    ins = nc.vector.tensor_tensor(x_res[:, t, :], src, x_res[:, t, :], ALU.add)
                ins.then_inc(s_out_read, 1)

            def statistics(b, layer, t, base):
                dve.wait_ge(s_out_read, b * 3 * LN + (layer - 1) * NT + t + 1)
                step(base, nc.vector.bn_stats(stat[:, t % 2, :], x_res[:, t, :]))
                hold()
                step(base, nc.vector.bn_aggr(mv[:, t, :], stat[:, t % 2, :]))
                nc.vector.tensor_scalar(ve[:, t:t + 1], mv[:, t, 1:2], LN_EPS, None, ALU.add).then_inc(s_var, 1)

            def normalize(b, layer, t):
                dve.wait_ge(s_rstd, b * 3 * LN + (layer - 1) * LN + t + 1)
                nc.vector.tensor_scalar(x_res[:, t, :], x_res[:, t, :], mv[:, t, 0:1], rstd[:, t:t + 1],
                                        ALU.subtract, ALU.mult).then_inc(s_y, 1)

            def normalize0(b, t):
                dve.wait_ge(s_x_in[t], b * (32 if t == 0 else 16) + (32 if t == 0 else 16))
                nc.vector.tensor_scalar(x_res[:, t, :], x_res[:, t, :], mv0[:, t, 0:1], rstd0[:, t:t + 1],
                                        ALU.subtract, ALU.mult).then_inc(s_y0, 1)

            def attention_sums(b, t, base):
                raw_counts = ((NT // 2) * 16 + 16, (NT // 2) * 16)[t % 2]
                done = 16 * (t // 2 + 1) + (16 if t % 2 == 0 else 0)
                dve.wait_ge(s_raw_in[t % 2], b * raw_counts + done)
                src = x_raw[:, t % 2, :]
                step(base, nc.vector.bn_stats(stat0[:, t % 2, :], src))
                hold()
                step(base, nc.vector.bn_aggr(mv0[:, t, :], stat0[:, t % 2, :]))
                mean = mv0[:, t, 0:1]
                step(base, nc.vector.scalar_tensor_tensor(out=prod, in0=src, scalar=mean, in1=v_rows[:, 0, :],
                                                          op0=ALU.subtract, op1=ALU.mult, accum_out=qi[:, t:t + 1]))
                ins = nc.vector.scalar_tensor_tensor(out=prod, in0=src, scalar=mean, in1=v_rows[:, 1, :],
                                                     op0=ALU.subtract, op1=ALU.mult, accum_out=qj[:, t:t + 1])
                ins.then_inc(s_raw_used, 1)

            def attention_columns(b, base):
                dve.wait_ge(s_raw_used, (b + 1) * NT)
                nc.vector.tensor_scalar(ve0[:], mv0[:, :, 1], LN_EPS, None, ALU.add).then_inc(s_var0, 1)
                dve.wait_ge(s_rstd0, b + 1)
                step(base, nc.vector.tensor_tensor(aj[:], qj[:], rstd0[:], ALU.mult))
                step(base, nc.vector.tensor_tensor(ai[:], qi[:], rstd0[:], ALU.mult))
                nc.vector.tensor_scalar(aj[:], aj[:], c_cols[:, 1:2], None, ALU.add).then_inc(s_aj, 1)
                step(base, nc.vector.tensor_scalar(ai[:], ai[:], c_cols[:, 0:1], None, ALU.add))
                step(base, nc.vector.tensor_scalar(shift[:], ai[:], SLOPE - 1.0, None, ALU.mult))
                step(base, nc.vector.tensor_scalar(floor[:], ai[:], -1.0, SINK, ALU.mult, ALU.add))

            def scores(b, t, base):
                dve.wait_ge(s_att_in[t], (b + 1) * 16)
                step(base, nc.vector.tensor_scalar(neg_mask[:], att[:, t, :], 0.0, MASKED, ALU.is_le, ALU.mult))
                step(base, nc.vector.scalar_tensor_tensor(out=att[:, t, :], in0=aj_row2[:], scalar=shift[:, t:t + 1],
                                                          in1=aj_row[:], op0=ALU.add, op1=ALU.max))
                hold()
                nc.vector.tensor_tensor_reduce(out=att[:, t, :], in0=att[:, t, :], in1=neg_mask[:],
                                               scale=1.0, scalar=-3.0e38, op0=ALU.add, op1=ALU.max,
                                               accum_out=top[:, t:t + 1]).then_inc(s_masked, 1)
                dve.wait_ge(s_masked, b * NT + t + 1)
                nc.vector.tensor_scalar(neg_top[:, t:t + 1], top[:, t:t + 1], floor[:, t:t + 1], -1.0,
                                        ALU.max, ALU.mult).then_inc(s_top, 1)

            def denominators(b, base):
                dve.wait_ge(s_top, (b + 1) * NT)
                nc.vector.tensor_tensor(sink_arg[:], floor[:], neg_top[:], ALU.add).then_inc(s_sink_arg, 1)
                dve.wait_ge(s_exp, (b + 1) * NT)
                dve.wait_ge(s_sink, b + 1)
                step(base, nc.vector.tensor_tensor(den[:], total[:], sink[:], ALU.add))
                step(base, nc.vector.reciprocal(rden[:], den[:]))
                nc.vector.tensor_tensor(covered[:], total[:], rden[:], ALU.mult).then_inc(s_den, 1)

            def mean_square(b, last, q):
                dve.wait_ge(s_turned[0], turn(b, last, TURN_RMS + q + 1))
                nc.vector.tensor_scalar(ms[:, q % 2, :], turn_bank[0][:, 0:2], 1.0 / HID3, RMS_EPS, ALU.mult, ALU.add)\
                  .then_inc(s_turn_free[0], 1)

            def hidden(b, q, m):
                i = NQ * HT2 + q * HT3 + m
                dve.wait_ge(s_hid_mm, b * HID + i + 1)
                nc.vector.tensor_scalar(hid[:, q % 2, m, :], hid_bank[i % 2][:, 0:QUARTER], b13[:, m:m + 1], None,
                                        ALU.add).then_inc(s_hid3, 1)

            def scale_hidden(b, last, q, m):
                if m == 0:
                    dve.wait_ge(s_turned[1], turn(b, last, TURN_RMS + q + 1))
                dve.wait_ge(s_hid_act, b * HID + NQ * HT2 + q * HT3 + m + 1)
                h = hid[:, q % 2, m, :]
                ins = nc.vector.scalar_tensor_tensor(out=h, in0=h, scalar=rms_col[:, m:m + 1],
                                                     in1=turn_bank[1][:, 0:QUARTER], op0=ALU.mult, op1=ALU.mult)
                ins.then_inc(s_scaled, 1)

            def graph(b, last, base):
                for k in range(NT):
                    if k >= 1:
                        turn_lo(b, last, k, k)
                    if k + 2 < NT:
                        normalize0(b, k + 2)
                    if k >= 4 and not last:
                        attention_sums(b + 1, k - 4, base)
                agg_lo(b, 1, 0)
                turn_lo(b, last, adj_use(0), 0)
                for t in range(NT // 2):
                    residual(b, 1, t)
                agg_lo(b, 1, 1)
                turn_lo(b, last, adj_use(1), 1)
                statistics(b, 1, 0, base)
                statistics(b, 1, 1, base)
                for t in range(NT // 2, NT):
                    residual(b, 1, t)
                normalize(b, 1, 0)
                normalize(b, 1, 1)
                statistics(b, 1, 2, base)
                statistics(b, 1, 3, base)
                for t in range(2, NT):
                    turn_lo(b, last, adj_use(t), t)
                    normalize(b, 1, t)
                    if t + 2 < NT:
                        statistics(b, 1, t + 2, base)
                    if t < 6 and not last:
                        attention_sums(b + 1, t + 2, base)
                if not last:
                    attention_columns(b + 1, base)
                agg_lo(b, 2, 0)
                if not last:
                    aj_scaled(split_count(b, last, TURN_AJ))
                    dve.wait_ge(s_turn_free[0], turn(b, last, TURN_AJ + 1))
                    dve.wait_ge(s_turn_free[1], split_count(b, last, TURN_AJ + 1))
                    scores(b + 1, 0, base)
                agg_lo(b, 2, 1)
                for q in range(NQ):
                    residual(b, 2, 2 * q)
                    residual(b, 2, 2 * q + 1)
                    statistics(b, 2, 2 * q, base)
                    statistics(b, 2, 2 * q + 1, base)
                    normalize(b, 2, 2 * q)
                    normalize(b, 2, 2 * q + 1)
                    if not last and q < NQ - 1:
                        scores(b + 1, q + 1, base)
                if not last:
                    for t in range(4, NT):
                        scores(b + 1, t, base)
                agg_lo(b, 3, 0)
                if not last:
                    denominators(b + 1, base)
                for q in range(NQ):
                    if q >= 2:
                        residual(b, 3, 2 * q - 4)
                        residual(b, 3, 2 * q - 3)
                    for m in range(HT3):
                        hidden(b, q, m)
                        if q >= 1 and m == sum_at(q):
                            mean_square(b, last, q - 1)
                        if q >= 1 and m > row_at(q):
                            scale_hidden(b, last, q - 1, m - row_at(q) - 1)
                    if q == 1:
                        agg_lo(b, 3, 1)
                    if q >= 1:
                        for m in range(HT3 - row_at(q) - 1, HT3):
                            scale_hidden(b, last, q - 1, m)
                    if q >= 2:
                        for t in (2 * q - 4, 2 * q - 3):
                            statistics(b, 3, t, base)
                        if q == NQ - 1:
                            mean_square(b, last, q)
                        for t in (2 * q - 4, 2 * q - 3):
                            normalize(b, 3, t)
                for m in range(HT3):
                    scale_hidden(b, last, NQ - 1, m)
                    if m == 1:
                        residual(b, 3, NT - 4)
                        residual(b, 3, NT - 3)
                if not last:
                    normalize0(b + 1, 0)
                    normalize0(b + 1, 1)
                for t in (NT - 4, NT - 3):
                    statistics(b, 3, t, base)
                for t in (NT - 4, NT - 3):
                    normalize(b, 3, t)
                if not last:
                    turn_lo(b + 1, False, 0, 0)
                for t in (NT - 2, NT - 1):
                    residual(b, 3, t)
                for t in (NT - 2, NT - 1):
                    statistics(b, 3, t, base)
                for t in (NT - 2, NT - 1):
                    normalize(b, 3, t)

            for t in range(NT):
                attention_sums(0, t, 0)
            attention_columns(0, 0)
            aj_scaled(0)
            for i in range(2):
                dve.wait_ge(s_turn_free[i], 1)
            for t in range(NT):
                scores(0, t, 0)
            denominators(0, 0)
            normalize0(0, 0)
            normalize0(0, 1)
            turn_lo(0, False, 0, 0)
            assert taken[0] == STEPS_FIRST
            with dve.Fori(0, GRAPHS - 1) as b:
                taken[0] = 0
                graph(b, False, b * STEPS + STEPS_FIRST)
                assert taken[0] == STEPS
            taken[0] = 0
            graph(GRAPHS - 1, True, (GRAPHS - 1) * STEPS + STEPS_FIRST)


_INS = ['x', 'adj', 'L0_gnn_W1', 'L0_gnn_b1', 'L0_gnn_W2', 'L0_gnn_b2', 'L0_gnn_fusion_w', 'L1_gnn_W',
        'L1_gnn_bW', 'L1_gnn_wai', 'L1_gnn_bai', 'L1_gnn_waj', 'L1_gnn_baj', 'L2_gnn_eps', 'L2_gnn_W1',
        'L2_gnn_b1', 'L2_gnn_W2', 'L2_gnn_b2', 'L3_gnn_epsilon', 'L3_gnn_W1', 'L3_gnn_b1',
        'L3_gnn_rms_weight', 'L3_gnn_W2', 'L3_gnn_b2']


def kernel(**inputs):
    import numpy as _np
    import concourse.bacc as _bacc
    from concourse import mybir as _mybir
    from concourse.bass_utils import run_bass_kernel_spmd as _run

    nc = _bacc.Bacc("TRN2", target_bir_lowering=False, num_devices=1, dynamic_dma_scratch_size=1024)
    arrays, args = {}, []
    for name in _INS:
        a = _np.ascontiguousarray(inputs[name])
        if name == 'L3_gnn_epsilon':
            a = a.reshape(1)
        arrays[f"in_{name}"] = a
        args.append(nc.dram_tensor(f"in_{name}", a.shape, _mybir.dt.from_np(a.dtype), kind="ExternalInput").ap())
    out = nc.dram_tensor("out", (GRAPHS, NODES, D), F32, kind="ExternalOutput").ap()
    adj_resnorm(nc, *args, out)
    r = _run(nc, [arrays], core_ids=[0])
    return r.results[0]["out"]
```
